# Optimizing a Trainium2 kernel written in Bass

```python
import numpy as np
import jax
import jax.numpy as jnp

def _softmax(x, axis=-1):
    return jax.nn.softmax(x, axis=axis)

def _gelu(x):
    return jax.nn.gelu(x, approximate=True)

def _silu(x):
    return jax.nn.silu(x)

def _sigmoid(x):
    return jax.nn.sigmoid(x)

def _layernorm(x, axis=-1, eps=1e-05):
    m = jnp.mean(x, axis=axis, keepdims=True)
    v = jnp.var(x, axis=axis, keepdims=True)
    return (x - m) / jnp.sqrt(v + eps)

def _scatter_add(tgt, idx, src, axis=0):
    return tgt.at[idx].add(src)

def _segment_sum(src, seg, n):
    return jax.ops.segment_sum(src, seg, n)
kernel_name = 'mk_xattn_seq_d2_seqx_r4_8b08bb'

def setup_inputs(seed: int=0):
    np.random.seed(seed)
    _w = jnp.asarray

    def _rec_inputs():
        import jax
        import jax.numpy as jnp
        _rk = jax.random.key(seed)
        x = 7.22e-05 + 1 * jax.random.normal(jax.random.fold_in(_rk, 1), (8, 112, 512), jnp.float32)
        _lenS = 112 - jax.random.randint(jax.random.fold_in(_rk, 7), (8,), 0, max(1, 112 // 4) + 1, jnp.int32)
        _lenS2 = 375 - jax.random.randint(jax.random.fold_in(_rk, 8), (8,), 0, max(1, 375 // 4) + 1, jnp.int32)
        _ctx_2048P = jax.random.normal(jax.random.fold_in(_rk, 11), (8, 16, 512), jnp.float32)
        _ctx_2048c = jax.random.dirichlet(jax.random.fold_in(_rk, 511), 0.3 * jnp.ones((16,), jnp.float32), (8, 375))
        _ctx_2048t = jnp.einsum('bsk,bkd->bsd', _ctx_2048c, _ctx_2048P)
        _ctx_2048t = _ctx_2048t * jax.lax.rsqrt(jnp.mean(jnp.square(_ctx_2048t)) + 1e-12) * 0.953939
        ctx_2048 = 2.81802e-05 + 1.00001 * (_ctx_2048t + 0.3 * jax.random.normal(jax.random.fold_in(_rk, 611), (8, 375, 512), jnp.float32))
        _validS = jnp.arange(112)[None, :] < _lenS[:, None]
        _validS2 = jnp.arange(375)[None, :] < _lenS2[:, None]
        _causal = jnp.tril(jnp.ones((112, 112), dtype=bool))
        mask_BxS2_bf1 = jnp.ones((8, 375), dtype=bool)
        return (x, ctx_2048, mask_BxS2_bf1)
    x, ctx_2048, mask_BxS2_bf1 = _rec_inputs()

    def _L0_xattn_setup():
        import jax, jax.numpy as jnp
        import numpy as np
        D = 512
        H = 16
        HD = D // H
        INNER = 4 * D
        EPS = 1e-05

        def layer_norm(x, w, b):
            mu = jnp.mean(x, axis=-1, keepdims=True)
            var = jnp.mean(jnp.square(x - mu), axis=-1, keepdims=True)
            return (x - mu) * jax.lax.rsqrt(var + EPS) * w + b
        key = jax.random.key(seed)
        ks = jax.random.split(key, 12)
        B, LQ, LK = (4, 256, 512)
        std = 0.02
        inp = {'hidden_states': jax.random.normal(ks[0], (B, LQ, D), jnp.float32), 'encoder_hidden_states': jax.random.normal(ks[1], (B, LK, D), jnp.float32), 'encoder_attention_mask': jnp.ones((B, LK), dtype=bool), 'ln1_w': jnp.ones((D,), jnp.float32), 'ln1_b': jnp.zeros((D,), jnp.float32), 'q_w': jax.random.normal(ks[2], (D, D), jnp.float32) * std, 'q_b': jnp.zeros((D,), jnp.float32), 'k_w': jax.random.normal(ks[3], (D, D), jnp.float32) * std, 'k_b': jnp.zeros((D,), jnp.float32), 'v_w': jax.random.normal(ks[4], (D, D), jnp.float32) * std, 'v_b': jnp.zeros((D,), jnp.float32), 'cproj_w': jax.random.normal(ks[5], (D, D), jnp.float32) * std, 'cproj_b': jnp.zeros((D,), jnp.float32), 'ln2_w': jnp.ones((D,), jnp.float32), 'ln2_b': jnp.zeros((D,), jnp.float32), 'fc_w': jax.random.normal(ks[6], (D, INNER), jnp.float32) * std, 'fc_b': jnp.zeros((INNER,), jnp.float32), 'proj_w': jax.random.normal(ks[7], (INNER, D), jnp.float32) * std, 'proj_b': jnp.zeros((D,), jnp.float32)}
        return inp
    _L0_xattn_all = _L0_xattn_setup()
    _L0_xattn_in = {k: v for k, v in _L0_xattn_all.items() if k in ('ln1_w', 'ln1_b', 'q_w', 'q_b', 'k_w', 'k_b', 'v_w', 'v_b', 'cproj_w', 'cproj_b', 'ln2_w', 'ln2_b', 'fc_w', 'fc_b', 'proj_w', 'proj_b')}
    del _L0_xattn_all

    def _L1_xattn_setup():
        import jax, jax.numpy as jnp
        import numpy as np
        B, Q, S1, S2 = (4, 64, 512, 512)
        D, H, K, F = (512, 16, 128, 2048)
        LN_EPS = 1e-05

        def _layer_norm(x, scale, offset):
            mu = jnp.mean(x, axis=-1, keepdims=True)
            var = jnp.var(x, axis=-1, keepdims=True)
            return (x - mu) * jax.lax.rsqrt(var + LN_EPS) * scale + offset

        def _cross_attention(q_in, kv_in, wq, bq, wk, bk, wv, bv, wo, bo, bias_k, bias_v):
            b, q_len, _ = q_in.shape
            t = kv_in.shape[1]
            qh = (q_in @ wq + bq).reshape(b, q_len, H, K)
            kh = (kv_in @ wk + bk).reshape(b, t, H, K)
            vh = (kv_in @ wv + bv).reshape(b, t, H, K)
            kh = jnp.concatenate([kh, jnp.broadcast_to(bias_k, (b, 1, H, K))], axis=1)
            vh = jnp.concatenate([vh, jnp.broadcast_to(bias_v, (b, 1, H, K))], axis=1)
            scale = jnp.sqrt(jnp.asarray(K, q_in.dtype))
            logits = jnp.einsum('bqhk,bthk->bhqt', qh, kh) / scale
            weights = jax.nn.softmax(logits, axis=-1)
            ctx = jnp.einsum('bhqt,bthk->bqhk', weights, vh).reshape(b, q_len, H * K)
            return ctx @ wo + bo

        def _forward(x, xf_1, xf_2, ln1_scale, ln1_offset, wq1, bq1, wk1, bk1, wv1, bv1, wo1, bo1, bias_k1, bias_v1, ln2_scale, ln2_offset, wq2, bq2, wk2, bk2, wv2, bv2, wo2, bo2, bias_k2, bias_v2, ln_mlp_scale, ln_mlp_offset, w_fc1, b_fc1, w_fc2, b_fc2):
            res = x
            h = _layer_norm(x, ln1_scale, ln1_offset)
            x = res + _cross_attention(h, xf_1, wq1, bq1, wk1, bk1, wv1, bv1, wo1, bo1, bias_k1, bias_v1)
            res = x
            h = _layer_norm(x, ln2_scale, ln2_offset)
            x = res + _cross_attention(h, xf_2, wq2, bq2, wk2, bk2, wv2, bv2, wo2, bo2, bias_k2, bias_v2)
            h = _layer_norm(x, ln_mlp_scale, ln_mlp_offset)
            h = jax.nn.gelu(h @ w_fc1 + b_fc1, approximate=False) @ w_fc2 + b_fc2
            return x + h
        key = jax.random.key(seed)
        ks = iter(jax.random.split(key, 64))

        def rn(shape, s=0.02):
            return jax.random.normal(next(ks), shape, jnp.float32) * s
        inp = {'x': rn((B, Q, D), 1.0), 'xf_1': rn((B, S1, D), 1.0), 'xf_2': rn((B, S2, D), 1.0)}
        for i in (1, 2):
            inp[f'ln{i}_scale'] = jnp.ones((D,), jnp.float32)
            inp[f'ln{i}_offset'] = jnp.zeros((D,), jnp.float32)
            inp[f'wq{i}'] = rn((D, H * K))
            inp[f'bq{i}'] = jnp.zeros((H * K,), jnp.float32)
            inp[f'wk{i}'] = rn((D, H * K))
            inp[f'bk{i}'] = jnp.zeros((H * K,), jnp.float32)
            inp[f'wv{i}'] = rn((D, H * K))
            inp[f'bv{i}'] = jnp.zeros((H * K,), jnp.float32)
            inp[f'wo{i}'] = rn((H * K, D))
            inp[f'bo{i}'] = jnp.zeros((D,), jnp.float32)
            inp[f'bias_k{i}'] = rn((1, 1, H, K))
            inp[f'bias_v{i}'] = rn((1, 1, H, K))
        inp['ln_mlp_scale'] = jnp.ones((D,), jnp.float32)
        inp['ln_mlp_offset'] = jnp.zeros((D,), jnp.float32)
        inp['w_fc1'] = rn((D, F))
        inp['b_fc1'] = jnp.zeros((F,), jnp.float32)
        inp['w_fc2'] = rn((F, D))
        inp['b_fc2'] = jnp.zeros((D,), jnp.float32)
        return inp
    _L1_xattn_all = _L1_xattn_setup()
    _L1_xattn_in = {k: v for k, v in _L1_xattn_all.items() if k in ('ln1_scale', 'ln1_offset', 'wq1', 'bq1', 'wk1', 'bk1', 'wv1', 'bv1', 'wo1', 'bo1', 'bias_k1', 'bias_v1', 'ln2_scale', 'ln2_offset', 'wq2', 'bq2', 'wk2', 'bk2', 'wv2', 'bv2', 'wo2', 'bo2', 'bias_k2', 'bias_v2', 'ln_mlp_scale', 'ln_mlp_offset', 'w_fc1', 'b_fc1', 'w_fc2', 'b_fc2')}
    del _L1_xattn_all
    return {'x': x, 'ctx_2048': ctx_2048, 'mask_BxS2_bf1': mask_BxS2_bf1, 'L0_xattn_ln1_w': _L0_xattn_in['ln1_w'], 'L0_xattn_ln1_b': _L0_xattn_in['ln1_b'], 'L0_xattn_q_w': _L0_xattn_in['q_w'], 'L0_xattn_q_b': _L0_xattn_in['q_b'], 'L0_xattn_k_w': _L0_xattn_in['k_w'], 'L0_xattn_k_b': _L0_xattn_in['k_b'], 'L0_xattn_v_w': _L0_xattn_in['v_w'], 'L0_xattn_v_b': _L0_xattn_in['v_b'], 'L0_xattn_cproj_w': _L0_xattn_in['cproj_w'], 'L0_xattn_cproj_b': _L0_xattn_in['cproj_b'], 'L0_xattn_ln2_w': _L0_xattn_in['ln2_w'], 'L0_xattn_ln2_b': _L0_xattn_in['ln2_b'], 'L0_xattn_fc_w': _L0_xattn_in['fc_w'], 'L0_xattn_fc_b': _L0_xattn_in['fc_b'], 'L0_xattn_proj_w': _L0_xattn_in['proj_w'], 'L0_xattn_proj_b': _L0_xattn_in['proj_b'], 'L1_xattn_ln1_scale': _L1_xattn_in['ln1_scale'], 'L1_xattn_ln1_offset': _L1_xattn_in['ln1_offset'], 'L1_xattn_wq1': _L1_xattn_in['wq1'], 'L1_xattn_bq1': _L1_xattn_in['bq1'], 'L1_xattn_wk1': _L1_xattn_in['wk1'], 'L1_xattn_bk1': _L1_xattn_in['bk1'], 'L1_xattn_wv1': _L1_xattn_in['wv1'], 'L1_xattn_bv1': _L1_xattn_in['bv1'], 'L1_xattn_wo1': _L1_xattn_in['wo1'], 'L1_xattn_bo1': _L1_xattn_in['bo1'], 'L1_xattn_bias_k1': _L1_xattn_in['bias_k1'], 'L1_xattn_bias_v1': _L1_xattn_in['bias_v1'], 'L1_xattn_ln2_scale': _L1_xattn_in['ln2_scale'], 'L1_xattn_ln2_offset': _L1_xattn_in['ln2_offset'], 'L1_xattn_wq2': _L1_xattn_in['wq2'], 'L1_xattn_bq2': _L1_xattn_in['bq2'], 'L1_xattn_wk2': _L1_xattn_in['wk2'], 'L1_xattn_bk2': _L1_xattn_in['bk2'], 'L1_xattn_wv2': _L1_xattn_in['wv2'], 'L1_xattn_bv2': _L1_xattn_in['bv2'], 'L1_xattn_wo2': _L1_xattn_in['wo2'], 'L1_xattn_bo2': _L1_xattn_in['bo2'], 'L1_xattn_bias_k2': _L1_xattn_in['bias_k2'], 'L1_xattn_bias_v2': _L1_xattn_in['bias_v2'], 'L1_xattn_ln_mlp_scale': _L1_xattn_in['ln_mlp_scale'], 'L1_xattn_ln_mlp_offset': _L1_xattn_in['ln_mlp_offset'], 'L1_xattn_w_fc1': _L1_xattn_in['w_fc1'], 'L1_xattn_b_fc1': _L1_xattn_in['b_fc1'], 'L1_xattn_w_fc2': _L1_xattn_in['w_fc2'], 'L1_xattn_b_fc2': _L1_xattn_in['b_fc2']}

def reference(x, ctx_2048, mask_BxS2_bf1, L0_xattn_ln1_w, L0_xattn_ln1_b, L0_xattn_q_w, L0_xattn_q_b, L0_xattn_k_w, L0_xattn_k_b, L0_xattn_v_w, L0_xattn_v_b, L0_xattn_cproj_w, L0_xattn_cproj_b, L0_xattn_ln2_w, L0_xattn_ln2_b, L0_xattn_fc_w, L0_xattn_fc_b, L0_xattn_proj_w, L0_xattn_proj_b, L1_xattn_ln1_scale, L1_xattn_ln1_offset, L1_xattn_wq1, L1_xattn_bq1, L1_xattn_wk1, L1_xattn_bk1, L1_xattn_wv1, L1_xattn_bv1, L1_xattn_wo1, L1_xattn_bo1, L1_xattn_bias_k1, L1_xattn_bias_v1, L1_xattn_ln2_scale, L1_xattn_ln2_offset, L1_xattn_wq2, L1_xattn_bq2, L1_xattn_wk2, L1_xattn_bk2, L1_xattn_wv2, L1_xattn_bv2, L1_xattn_wo2, L1_xattn_bo2, L1_xattn_bias_k2, L1_xattn_bias_v2, L1_xattn_ln_mlp_scale, L1_xattn_ln_mlp_offset, L1_xattn_w_fc1, L1_xattn_b_fc1, L1_xattn_w_fc2, L1_xattn_b_fc2):
    import jax
    import jax.numpy as jnp

    def _L0_xattn_ref(hidden_states, encoder_hidden_states, encoder_attention_mask, ln1_w, ln1_b, q_w, q_b, k_w, k_b, v_w, v_b, cproj_w, cproj_b, ln2_w, ln2_b, fc_w, fc_b, proj_w, proj_b):
        import jax, jax.numpy as jnp
        import numpy as np
        D = 512
        H = 16
        HD = D // H
        INNER = 4 * D
        EPS = 1e-05

        def layer_norm(x, w, b):
            mu = jnp.mean(x, axis=-1, keepdims=True)
            var = jnp.mean(jnp.square(x - mu), axis=-1, keepdims=True)
            return (x - mu) * jax.lax.rsqrt(var + EPS) * w + b
        B, LQ, _ = hidden_states.shape
        LK = encoder_hidden_states.shape[1]
        residual = hidden_states
        x = layer_norm(hidden_states, ln1_w, ln1_b)
        q = (x @ q_w + q_b).reshape(B, LQ, H, HD).transpose(0, 2, 1, 3)
        k = (encoder_hidden_states @ k_w + k_b).reshape(B, LK, H, HD).transpose(0, 2, 1, 3)
        v = (encoder_hidden_states @ v_w + v_b).reshape(B, LK, H, HD).transpose(0, 2, 1, 3)
        scale = 1.0 / np.sqrt(HD).astype(np.float32)
        scores = jnp.einsum('bhqd,bhkd->bhqk', q, k) * scale
        mask = encoder_attention_mask[:, None, None, :]
        mask_value = jnp.finfo(scores.dtype).min
        scores = jnp.where(mask, scores, mask_value)
        attn = jax.nn.softmax(scores, axis=-1)
        out = jnp.einsum('bhqk,bhkd->bhqd', attn, v)
        out = out.transpose(0, 2, 1, 3).reshape(B, LQ, D)
        out = out @ cproj_w + cproj_b
        hidden = out + residual
        residual = hidden
        y = layer_norm(hidden, ln2_w, ln2_b)
        y = jax.nn.gelu(y @ fc_w + fc_b, approximate=True)
        y = y @ proj_w + proj_b
        return residual + y

    def _L1_xattn_ref(x, xf_1, xf_2, ln1_scale, ln1_offset, wq1, bq1, wk1, bk1, wv1, bv1, wo1, bo1, bias_k1, bias_v1, ln2_scale, ln2_offset, wq2, bq2, wk2, bk2, wv2, bv2, wo2, bo2, bias_k2, bias_v2, ln_mlp_scale, ln_mlp_offset, w_fc1, b_fc1, w_fc2, b_fc2):
        import jax, jax.numpy as jnp
        import numpy as np
        B, Q, S1, S2 = (4, 64, 512, 512)
        D, H, K, F = (512, 16, 128, 2048)
        LN_EPS = 1e-05

        def _layer_norm(x, scale, offset):
            mu = jnp.mean(x, axis=-1, keepdims=True)
            var = jnp.var(x, axis=-1, keepdims=True)
            return (x - mu) * jax.lax.rsqrt(var + LN_EPS) * scale + offset

        def _cross_attention(q_in, kv_in, wq, bq, wk, bk, wv, bv, wo, bo, bias_k, bias_v):
            b, q_len, _ = q_in.shape
            t = kv_in.shape[1]
            qh = (q_in @ wq + bq).reshape(b, q_len, H, K)
            kh = (kv_in @ wk + bk).reshape(b, t, H, K)
            vh = (kv_in @ wv + bv).reshape(b, t, H, K)
            kh = jnp.concatenate([kh, jnp.broadcast_to(bias_k, (b, 1, H, K))], axis=1)
            vh = jnp.concatenate([vh, jnp.broadcast_to(bias_v, (b, 1, H, K))], axis=1)
            scale = jnp.sqrt(jnp.asarray(K, q_in.dtype))
            logits = jnp.einsum('bqhk,bthk->bhqt', qh, kh) / scale
            weights = jax.nn.softmax(logits, axis=-1)
            ctx = jnp.einsum('bhqt,bthk->bqhk', weights, vh).reshape(b, q_len, H * K)
            return ctx @ wo + bo

        def _forward(x, xf_1, xf_2, ln1_scale, ln1_offset, wq1, bq1, wk1, bk1, wv1, bv1, wo1, bo1, bias_k1, bias_v1, ln2_scale, ln2_offset, wq2, bq2, wk2, bk2, wv2, bv2, wo2, bo2, bias_k2, bias_v2, ln_mlp_scale, ln_mlp_offset, w_fc1, b_fc1, w_fc2, b_fc2):
            res = x
            h = _layer_norm(x, ln1_scale, ln1_offset)
            x = res + _cross_attention(h, xf_1, wq1, bq1, wk1, bk1, wv1, bv1, wo1, bo1, bias_k1, bias_v1)
            res = x
            h = _layer_norm(x, ln2_scale, ln2_offset)
            x = res + _cross_attention(h, xf_2, wq2, bq2, wk2, bk2, wv2, bv2, wo2, bo2, bias_k2, bias_v2)
            h = _layer_norm(x, ln_mlp_scale, ln_mlp_offset)
            h = jax.nn.gelu(h @ w_fc1 + b_fc1, approximate=False) @ w_fc2 + b_fc2
            return x + h
        return _forward(x, xf_1, xf_2, ln1_scale, ln1_offset, wq1, bq1, wk1, bk1, wv1, bv1, wo1, bo1, bias_k1, bias_v1, ln2_scale, ln2_offset, wq2, bq2, wk2, bk2, wv2, bv2, wo2, bo2, bias_k2, bias_v2, ln_mlp_scale, ln_mlp_offset, w_fc1, b_fc1, w_fc2, b_fc2)
    x = _L0_xattn_ref(x, ctx_2048, mask_BxS2_bf1, L0_xattn_ln1_w, L0_xattn_ln1_b, L0_xattn_q_w, L0_xattn_q_b, L0_xattn_k_w, L0_xattn_k_b, L0_xattn_v_w, L0_xattn_v_b, L0_xattn_cproj_w, L0_xattn_cproj_b, L0_xattn_ln2_w, L0_xattn_ln2_b, L0_xattn_fc_w, L0_xattn_fc_b, L0_xattn_proj_w, L0_xattn_proj_b)
    x = _L1_xattn_ref(x, ctx_2048, ctx_2048, L1_xattn_ln1_scale, L1_xattn_ln1_offset, L1_xattn_wq1, L1_xattn_bq1, L1_xattn_wk1, L1_xattn_bk1, L1_xattn_wv1, L1_xattn_bv1, L1_xattn_wo1, L1_xattn_bo1, L1_xattn_bias_k1, L1_xattn_bias_v1, L1_xattn_ln2_scale, L1_xattn_ln2_offset, L1_xattn_wq2, L1_xattn_bq2, L1_xattn_wk2, L1_xattn_bk2, L1_xattn_wv2, L1_xattn_bv2, L1_xattn_wo2, L1_xattn_bo2, L1_xattn_bias_k2, L1_xattn_bias_v2, L1_xattn_ln_mlp_scale, L1_xattn_ln_mlp_offset, L1_xattn_w_fc1, L1_xattn_b_fc1, L1_xattn_w_fc2, L1_xattn_b_fc2)
    return x

_drawn_inputs = setup_inputs


def setup_inputs(seed=0):
    import zlib

    import numpy as np

    out = dict(_drawn_inputs(seed))
    spreads = {'L0_xattn_ln1_w': (1.0, 0.6),
     'L0_xattn_ln1_b': (0.0, 0.8),
     'L0_xattn_q_b': (0.0, 0.8),
     'L0_xattn_k_b': (0.0, 2.0),
     'L0_xattn_v_b': (0.0, 0.1),
     'L0_xattn_cproj_b': (0.0, 0.1),
     'L0_xattn_ln2_w': (1.0, 0.2),
     'L0_xattn_ln2_b': (0.0, 0.36),
     'L0_xattn_fc_b': (0.0, 0.1),
     'L0_xattn_proj_b': (0.0, 0.1),
     'L1_xattn_ln1_scale': (1.0, 0.6),
     'L1_xattn_ln1_offset': (0.0, 0.8),
     'L1_xattn_bq1': (0.0, 0.8),
     'L1_xattn_bk1': (0.0, 2.0),
     'L1_xattn_bv1': (0.0, 0.1),
     'L1_xattn_bo1': (0.0, 0.1),
     'L1_xattn_ln2_scale': (1.0, 0.6),
     'L1_xattn_ln2_offset': (0.0, 0.8),
     'L1_xattn_bq2': (0.0, 0.8),
     'L1_xattn_bk2': (0.0, 2.0),
     'L1_xattn_bv2': (0.0, 0.1),
     'L1_xattn_bo2': (0.0, 0.1),
     'L1_xattn_ln_mlp_scale': (1.0, 0.2),
     'L1_xattn_ln_mlp_offset': (0.0, 0.362),
     'L1_xattn_b_fc1': (0.0, 0.1),
     'L1_xattn_b_fc2': (0.0, 0.1)}
    factors = {'L0_xattn_q_w': 7.807,
     'L0_xattn_k_w': 7.663,
     'L1_xattn_wq1': 4.054,
     'L1_xattn_wk1': 3.96,
     'L1_xattn_bias_k1': 64.0,
     'L1_xattn_bias_v1': 64.0,
     'L1_xattn_wq2': 4.058,
     'L1_xattn_wk2': 3.979,
     'L1_xattn_bias_k2': 64.0,
     'L1_xattn_bias_v2': 64.0}
    for name, (base, spread) in spreads.items():
        noise = np.random.default_rng([zlib.crc32(name.encode()), seed]).standard_normal(out[name].shape)
        drawn = base * np.exp(spread * noise) if base else spread * noise
        out[name] = jnp.asarray(drawn.astype(out[name].dtype))
    for name, factor in factors.items():
        out[name] = (out[name] * factor).astype(out[name].dtype)
    return out
```

```python
from contextlib import ExitStack

import concourse.bass as bass
from concourse import mybir

F32 = mybir.dt.float32
F32R = mybir.dt.float32r
U8 = mybir.dt.uint8
ACT = mybir.ActivationFunctionType
ALU = mybir.AluOpType
AX_X = mybir.AxisListType.X
ds = bass.ds

P = 128
NB = 8
LQ = 112
LK = 375
KW = LK + 1
D = 512
DT = D // P
ROWS = NB * LQ
RT = ROWS // P
HALF = ROWS // 2
KEY_TILES = [(0, 128), (128, 128), (256, LK - 256)]
GROUPS = 4
PAIRS = NB // 2
NT = 4
SUB0 = 4
HD0, HD1 = 32, 128
EPS = 1e-5
LARGEST = 3.4028234663852886e38

A_Q0, A_K0, A_O0, A_M0 = 0, 1, 2, 3
B_V0, B_M0 = 0, 1
A_L1, B_L1, PER_LAYER = 7, 5, 8
A_M1, B_M1 = A_L1 + 2 * PER_LAYER, B_L1 + 2 * PER_LAYER
N_A, N_B = A_M1 + 4, B_M1 + 4

C_BQ0, C_BK0, C_BV0, C_FC0, C_FC1, C_LN = 0, 4, 8, 12, 28, 44
N_CA = C_LN + 8 * 5
C_BQ1, C_BK1, C_BV1, C_XK1, N_CB1 = 0, 16, 32, 48, 64

OUT_CHUNKS = [(0, 4), (4, 3)]
MLP_CHUNKS = [(0, 384), (384, 256), (640, 256)]
CHUNK_MAX = 384


class Attention:

    def __init__(self, layer, sub, tile0, unit0, batch0):
        self.layer, self.sub = layer, sub
        self.tile0, self.unit0, self.batch0 = tile0, unit0, batch0
        self.score_ahead = 3 if layer == 0 else 2
        self.key_ahead, self.key_slot = (2, 2) if layer == 0 else (3, 0)
        self.context_slot = (2, 0) if layer == 0 else (1, 0)
        self.keys = LK if layer == 0 else KW

    def units_before(self, tile):
        return self.unit0 + self.sub * (tile - self.tile0)

    def vals(self):
        return [n if i < 2 else n + self.layer for i, (_, n) in enumerate(KEY_TILES)]


class Place:

    def __init__(self, att, a, group, pair, parity, final=False):
        self.att, self.a, self.group, self.pair, self.parity = att, a, group, pair, parity
        self.b = 2 * pair + parity
        self.swap = isinstance(self.b, int) and self.b == NB - 1
        self.final_pair = final
        self.final = final and self.swap
        blocks = a * GROUPS + group
        self.batch = att.batch0 + blocks * NB + self.b
        self.same_parity = att.batch0 // 2 + blocks * PAIRS + pair
        self.block = blocks
        self.tile = self.batch * NT
        self.unit = att.units_before(self.tile)
        self.block_a = A_K0 if att.layer == 0 else A_L1 + 2 + PER_LAYER * a + group
        self.block_b = B_V0 if att.layer == 0 else B_L1 + 2 + PER_LAYER * a + group

    def next(self):
        if self.swap:
            return Place(self.att, self.a, self.group + 1, 0, 0)
        if self.parity:
            return Place(self.att, self.a, self.group, self.pair + 1, 0, self.final_pair)
        return Place(self.att, self.a, self.group, self.pair, 1, self.final_pair)

    def key(self, t):
        if t < NT:
            return self, t
        return None if self.final else (self.next(), t - NT)

    def at(self, t, j, ahead):
        n = self.att.sub * t + j + ahead
        tile = self.key(n // self.att.sub)
        return tile and (*tile, n % self.att.sub)

    def after(self, batches):
        if batches == 0:
            return self
        return None if self.final else self.next().after(batches - 1)

    def column(self, kind, t):
        if self.att.layer == 0:
            return kind[0] + t
        return N_CB1 * self.a + kind[1] + NT * self.group + t


ATT0 = Attention(0, SUB0, 0, 0, 0)
ATT1 = Attention(1, 1, NB * NT, NB * NT * SUB0, NB)


def wait(eng, sem, value):
    if isinstance(value, int) and value <= 0:
        return
    eng.wait_ge(sem, value)


def build(nc, x_in, ctx_in, mask_in, blocks_a, blocks_b, vec_a, vec_b, value_rows, value_bias_rows, row_bias, eye, out):
    q_scr = [nc.dram_tensor(f"q_{s}_scratch", [GROUPS, NB, P, NT * LQ], F32).ap() for s in ("hi", "lo")]
    o_scr = [nc.dram_tensor(f"o_{s}_scratch", [GROUPS, NT, P, ROWS], F32).ap() for s in ("hi", "lo")]
    xv_scr = nc.dram_tensor("extra_value_scratch", [2, GROUPS, D], F32).ap()

    with ExitStack() as ctx:
        def sb(name, shape, dt=F32):
            return ctx.enter_context(nc.sbuf_tensor(name, shape, dt))

        def sem(name):
            return ctx.enter_context(nc.semaphore(name))

        ctx_t = sb("ctx_t", [P, DT, NB * KW])
        x = sb("x", [P, RT, D])
        ident = sb("ident", [P, P])
        col_a = sb("col_a", [P, N_CA])
        col_b = sb("col_b", [P, 2 * N_CB1])
        xk = [sb(f"xk_{s}", [P, 32], F32R) for s in ("hi", "lo")]
        bias_row = sb("bias_row", [P, D])
        mask_u8 = sb("mask_u8", [LQ, NB * LK], U8)
        key_cap = sb("key_cap", [LQ, LK])
        act_t = [sb(f"act_t_{s}", [P, DT, ROWS], F32R) for s in ("hi", "lo")]
        w_raw = [sb(f"w_raw_{s}", [P, DT, D]) for s in "ab"]
        w = [[sb(f"w_{s}_{h}", [P, DT, D], F32R) for h in ("hi", "lo")] for s in "ab"]
        cs = [[sb(f"cs{i}_{h}", [P, DT * CHUNK_MAX], F32R) for h in ("hi", "lo")] for i in range(2)]
        q = [[sb(f"q{i}_{h}", [P, NT * LQ], F32R) for h in ("hi", "lo")] for i in range(2)]
        v = [sb(f"v{i}", [P, 3, D]) for i in range(2)]
        k = [[sb(f"k{i}_{h}", [P, KW], F32R) for h in ("hi", "lo")] for i in range(2)]
        prob = [sb(f"prob{i}", [P, D]) for i in range(2)]
        prob_t = [sb(f"prob_t{i}", [P, 3 * LQ]) for i in range(2)]
        o = sb("o", [P, D])
        o_split = [sb(f"o_{h}", [P, NT * LQ], F32R) for h in ("hi", "lo")]
        stats = sb("stats", [P, RT, 6])
        mean_var = sb("mean_var", [P, RT, 2])
        var_eps = sb("var_eps", [P, RT])
        std = sb("std", [P, RT])
        rstd = sb("rstd", [P, RT])
        max_neg = sb("max_neg", [P, 2])
        prob_sum = sb("prob_sum", [P, 2])
        prob_rcp = sb("prob_rcp", [P, 2])

        def bank(name):
            return ctx.enter_context(nc.psum_tensor(name, [P, 512], F32))

        ps_k, ps_v = bank("ps_k"), bank("ps_v")
        ps_s = [bank(f"ps_s{i}") for i in range(2)]
        ps_t = [bank(f"ps_t{i}") for i in range(2)]
        ps_o = [bank(f"ps_o{i}") for i in range(2)]
        ps_y = [ps_k, ps_v]

        start_in, ctx_in_sem, vecs_in = sem("start_in"), sem("ctx_in"), sem("vecs_in")
        vec_t, vec_ev, vec_split, xv_diff, xv_out = (sem(n) for n in ("vec_t", "vec_ev", "vec_split", "xv_diff", "xv_out"))
        cleared = sem("cleared")
        w_in = [sem(f"w_in_{s}") for s in "ab"]
        w_hi = [sem(f"w_hi_{s}") for s in "ab"]
        w_lo = [sem(f"w_lo_{s}") for s in "ab"]
        ln_stat, ln_agg, ln_eps, ln_std, ln_rstd, ln_xhat, ln_turn, ln_act, ln_hi, ln_lo = (
            sem("ln_" + n) for n in ("stat", "agg", "eps", "std", "rstd", "xhat", "turn", "act", "hi", "lo"))
        bias_in, bias_add = sem("bias_in"), sem("bias_add")
        q_mm, q_act, q_hi, q_lo = (sem("q_" + n) for n in ("mm", "act", "hi", "lo"))
        q_out = [sem(f"q_out{i}") for i in range(2)]
        q_in = [sem(f"q_in{i}") for i in range(2)]
        cs_hi, cs_lo = sem("cs_hi"), sem("cs_lo")
        k_mm, k_hi, k_lo, k_extra = sem("k_mm"), sem("k_hi"), sem("k_lo"), sem("k_extra")
        v_mm, v_ev = sem("v_mm"), sem("v_ev")
        xv_in = [sem(f"xv_in{i}") for i in range(2)]
        s_mm, s_cap, s_max, s_exp, s_rcp, s_norm = (
            sem("s_" + n) for n in ("mm", "cap", "max", "exp", "rcp", "norm"))
        cap_half, cap_full = sem("cap_half"), sem("cap_full")
        t_mm, t_ev, av_mm = sem("t_mm"), sem("t_ev"), sem("av_mm")
        o_ev, o_hi, o_lo, o_out = sem("o_ev"), sem("o_hi"), sem("o_lo"), sem("o_out")
        o_in = [sem(f"o_in{i}") for i in range(2)]
        y_mm, x_add = sem("y_mm"), sem("x_add")
        h_mm, h_act, h_hi, h_lo = (sem("h_" + n) for n in ("mm", "act", "hi", "lo"))
        stored = sem("stored")
        act_waited, dve_waited, pool_waited, sp_waited = (sem(n + "_waited") for n in ("act", "dve", "pool", "sp"))

        block = ctx.enter_context(nc.Block())

        def schedule(eng, ln, query, attend, project, mlp, projected=None):
            ln(0, 0)
            query(0, 0, 0, 0, A_Q0, 0)
            attend(ATT0, 0)
            project(0, 0, 0, 0, A_O0, 0, 0)
            ln(1, RT)
            mlp(0, 0, 1, RT)
            with eng.Fori(1, 4) as fg:
                mlp(0, fg, 1, RT * (fg + 1))
            with eng.Fori(0, 2) as a:
                ln(2 + a, 5 * RT + 4 * RT * a)
                with eng.Fori(0, GROUPS // 2) as half:
                    for slot, first in ((0, A_L1), (1, B_L1)):
                        query(1, a, 2 * half + slot, slot, PER_LAYER * a + half + first, 1 + 4 * a + 2 * half + slot)
                attend(ATT1, a)
                with eng.Fori(0, GROUPS // 2) as half:
                    for slot, first in ((0, A_L1 + 6), (1, B_L1 + 6)):
                        project(1, a, 2 * half + slot, slot, PER_LAYER * a + half + first,
                                1 + 4 * a + 2 * half + slot, 5 * RT + 4 * RT * a + 2 * RT * half + RT * slot)
                if projected:
                    projected(a)
            ln(4, 13 * RT)
            with eng.Fori(0, 2) as fg:
                mlp(1, fg, 4, 13 * RT + RT * fg)
            mlp(1, 2, 4, 15 * RT)
            mlp(1, 3, 4, 16 * RT)

        def batches(eng, att, a, prologue, one_batch):
            def pair(group, p, final=False):
                for parity in range(2):
                    one_batch(Place(att, a, group, p, parity, final))

            prologue(Place(att, a, 0, 0, 0))
            if att.layer == 0:
                pair(0, 0)
                with eng.Fori(1, PAIRS - 1) as p:
                    pair(0, p)
                pair(0, PAIRS - 1, final=True)
                return
            with eng.Fori(0, GROUPS - 1) as group:
                with eng.Fori(0, PAIRS - 1) as p:
                    pair(group, p)
                pair(group, PAIRS - 1)
            with eng.Fori(0, PAIRS - 1) as p:
                pair(GROUPS - 1, p)
            pair(GROUPS - 1, PAIRS - 1, final=True)

        V_SLOTS = [{(1, 1): 0, (2, 1): 1, (3, 1): 2}, {(1, 0): 0, (2, 0): 1, (3, 0): 2}]

        def mlp_block(m, fg):
            return (A_M0, A_M1)[m] + fg, (B_M0, B_M1)[m] + fg

        def exists(slot, n):
            return not isinstance(n, int) or n < (N_A, N_B)[slot]

        def cols(att):
            return col_b if att.layer else col_a

        @block.sync
        def _(sp):
            def load_block(slot, n):
                if not exists(slot, n):
                    return
                wait(sp, w_lo[slot], 4 * n)
                src = (blocks_a, blocks_b)[slot][ds(n, 1)].rearrange("o p f -> (o p) f")
                sp.dma_start(w_raw[slot][:].rearrange("p k n -> p (k n)"), src).then_inc(w_in[slot], 16)

            def ln(e, x0):
                wait(sp, bias_add, RT * e)
                sp.dma_start(bias_row[:], row_bias[ds(e, 1), :].partition_broadcast(P)).then_inc(bias_in, 16)

            def query(layer, a, group, slot, n, step):
                for i in range(2 * NT):
                    t, half = i // 2, i % 2
                    sp.wait_ge(q_lo, 8 * step + i + 1)
                    for s in range(2):
                        src = cs[half][s][:, 0:HALF].bitcast(F32).rearrange("p (b r) -> p b r", b=NB // 2)
                        dst = q_scr[s][ds(group, 1), half * 4:half * 4 + 4, :, t * LQ:(t + 1) * LQ]
                        sp.dma_start(dst.rearrange("o b p r -> p (o b) r"), src).then_inc(q_out[half], 16)
                load_block(slot, n + 2)

            def load_q(place):
                wait(sp, s_mm, place.att.units_before(place.tile - NT))
                for s in range(2):
                    src = q_scr[s][ds(place.group, 1), ds(place.b, 1)].rearrange("g b p f -> (g b p) f")
                    sp.dma_start(q[place.parity][s][:].bitcast(F32), src).then_inc(q_in[place.parity], 16)

            def load_extra_value(place, buf):
                wait(sp, av_mm, place.att.units_before(place.tile - NT * (1 - buf)))
                src = xv_scr[ds(place.a, 1), ds(place.group, 1)].rearrange("a g f -> (a g) f")
                sp.dma_start(v[buf][LK - 256:LK - 255, 2, :], src).then_inc(xv_in[buf], 16)

            def attend(att, a):
                def prologue(place):
                    for half in range(2):
                        sp.wait_ge(q_out[half], 32 * NT * (1 + 4 * (a + 1) if att.layer else 1))
                    load_q(place)
                    if att.layer == 1:
                        for buf in range(2):
                            load_extra_value(place, buf)

                def one_batch(place):
                    after = None if place.final else place.next()
                    if after:
                        load_q(after)
                    if place.swap:
                        if after:
                            load_extra_value(after, 0)
                        load_block(0, place.block_a + 2)
                        if after or att.layer == 0:
                            load_block(1, place.block_b + 2)
                    sp.wait_ge(o_lo, place.batch + 1)
                    for s in range(2):
                        dst = o_scr[s][ds(place.group, 1), :, :, ds(place.b * LQ, LQ)].rearrange("g h p r -> p (g h) r")
                        sp.dma_start(dst, o_split[s][:].bitcast(F32).rearrange("p (h r) -> p h r", h=NT)).then_inc(o_out, 16)
                    if place.swap and after:
                        load_extra_value(after, 1)

                batches(sp, att, a, prologue, one_batch)

            def project(layer, a, group, slot, n, step, x0):
                for c, (r0, nr) in enumerate(OUT_CHUNKS):
                    wait(sp, y_mm, x0 - RT + r0 + nr)
                    sp.sem_inc(sp_waited, 1)
                    sp.wait_ge(o_out, 32 * NB * (1 + 4 * (a + 1) if layer else 1))
                    sp.sem_inc(sp_waited, 1)
                    for s in range(2):
                        src = o_scr[s][ds(group, 1), :, :, r0 * P:(r0 + nr) * P].rearrange("g h p r -> p (g h) r")
                        sp.dma_start(act_t[s][:, :, r0 * P:(r0 + nr) * P].bitcast(F32), src).then_inc(o_in[c], 16)
                    if c == 0 and layer:
                        load_block(1 - slot, n - B_L1 + A_L1 + 2 if slot else n - A_L1 + B_L1 + 1)
                if layer == 0:
                    load_block(slot, n + 2)

            def projected(a):
                load_block(1, B_L1 + 9 + PER_LAYER * a)

            def mlp(m, fg, e, x0):
                na, nb = mlp_block(m, fg)
                load_block(0, na + 2)
                load_block(1, nb + 2)
                if isinstance(fg, int) and m == 1 and fg == 3:
                    for r in range(RT):
                        sp.wait_ge(x_add, x0 + r + 1)
                        sp.dma_start(out[r * P:(r + 1) * P, :], x[:, r, :]).then_inc(stored, 16)
                    sp.wait_ge(stored, 16 * RT)

            sp.dma_start(x[:], x_in.rearrange("(r p) d -> p r d", p=P)).then_inc(start_in, 16)
            sp.dma_start(ident[:], eye).then_inc(vecs_in, 16)
            sp.dma_start(prob[0][0:N_CA, 0:P], vec_a).then_inc(vecs_in, 16)
            sp.dma_start(prob[0][:, P:2 * P], vec_b).then_inc(vecs_in, 16)
            sp.dma_start(prob[0][0:32, 2 * P:3 * P], value_rows).then_inc(vecs_in, 16)
            sp.dma_start(prob[0][0:32, 3 * P:4 * P], value_bias_rows).then_inc(vecs_in, 16)
            sp.dma_start(mask_u8[:], mask_in.partition_broadcast(LQ)).then_inc(vecs_in, 16)
            load_block(0, 0)
            load_block(1, 0)
            sp.dma_start(ctx_t[:].rearrange("p k n -> p (k n)"), ctx_in).then_inc(ctx_in_sem, 16)
            load_block(0, 1)
            load_block(1, 1)
            sp.wait_ge(xv_diff, 1)
            sp.dma_start(xv_scr.rearrange("a g (t n) -> (a g t) n", n=P), key_cap[0:32, 0:P]).then_inc(xv_out, 16)
            schedule(sp, ln, query, attend, project, mlp, projected)

        @block.gpsimd
        def _(pool):
            def ln(e, x0):
                pool.wait_ge(bias_in, 16 * e + 16)
                for r in range(RT):
                    pool.wait_ge(ln_xhat, RT * e + r + 1)
                    pool.tensor_tensor(x[:, r, :], x[:, r, :], bias_row[:], ALU.add).then_inc(bias_add, 1)

            def attend(att, a):
                def context_lo(place):
                    pool.wait_ge(cs_hi, place.batch + 1)
                    pool.tensor_tensor(cs[place.parity][1][:, 0:DT * KW].rearrange("p (k n) -> p k n", k=DT),
                                       ctx_t[:, :, ds(place.b * KW, KW)],
                                       cs[place.parity][0][:, 0:DT * KW].rearrange("p (k n) -> p k n", k=DT),
                                       ALU.subtract).then_inc(cs_lo, 1)

                def extra_key(place, t):
                    col = 16 * place.a + NT * place.group + t
                    wait(pool, s_mm, att.units_before(place.tile + t - 1))
                    pool.sem_inc(pool_waited, 1)
                    pool.tensor_copy(k[t % 2][0][:, LK:KW], xk[0][:, ds(col, 1)])
                    pool.tensor_copy(k[t % 2][1][:, LK:KW], xk[1][:, ds(col, 1)]).then_inc(k_extra, 1)

                def prologue(place):
                    pool.wait_ge(ctx_in_sem, 16)
                    context_lo(place)
                    context_lo(place.next())
                    if att.layer == 1:
                        for t in range(att.key_ahead):
                            extra_key(place, t)

                def one_batch(place):
                    for t in range(NT):
                        tile = place.key(t + att.key_ahead)
                        if att.layer == 1 and tile:
                            extra_key(*tile)
                        if t == att.context_slot[0] and place.after(2):
                            context_lo(place.after(2))

                batches(pool, att, a, prologue, one_batch)

            skip = lambda *_: None
            pool.wait_ge(vec_split, 2)
            schedule(pool, ln, skip, attend, skip, skip)

        @block.scalar
        def _(act):
            def split_hi(slot, n, subs, free):
                if not exists(slot, n):
                    return
                act.wait_ge(w_in[slot], 16 * n + 16)
                for s in subs:
                    if free:
                        act.wait_ge(*free(s))
                    act.activation(w[slot][0][:, :, s * P:(s + 1) * P], w_raw[slot][:, :, s * P:(s + 1) * P],
                                   ACT.Identity).then_inc(w_hi[slot], 1)

            def ln(e, x0):
                act.wait_ge(ln_eps, e + 1)
                act.activation(std[:], var_eps[:], ACT.Sqrt).then_inc(ln_std, 1)
                for r in range(RT):
                    act.wait_ge(ln_turn, RT * e + r + 1)
                    wait(act, ln_lo, RT * e + r)
                    act.sem_inc(act_waited, 1)
                    for c in range(DT):
                        last = act.activation(o[:, c * P:(c + 1) * P], ps_t[r % 2][:, c * P:(c + 1) * P], ACT.Identity,
                                              bias=col_a[:, ds(C_LN + 8 * e + 4 + c, 1)],
                                              scale=col_a[:, ds(C_LN + 8 * e + c, 1)])
                    last.then_inc(ln_act, 1)

            def query(layer, a, group, slot, n, step):
                scale = float((HD1 if layer else HD0) ** -0.5)
                for i in range(2 * NT):
                    t, half = i // 2, i % 2
                    col = (N_CB1 * a + C_BQ1 if layer else C_BQ0) + NT * group + t
                    act.wait_ge(q_mm, 8 * step + i + 1)
                    wait(act, q_lo, 8 * step + i - 1)
                    act.sem_inc(act_waited, 1)
                    act.activation(prob[half][:, 0:HALF], ps_y[half][:, 0:HALF], ACT.Identity, scale=scale,
                                   bias=(col_b if layer else col_a)[:, ds(col, 1)]).then_inc(q_act, 1)
                split_hi(slot, n + 1, range(4), lambda s: (q_mm, 8 * step + 2 * s + 2))

            def attend(att, a):
                sub, layer = att.sub, att.layer

                def key_hi(place, t):
                    tile = place.tile + t
                    act.wait_ge(k_mm, tile + 1)
                    wait(act, s_mm, att.units_before(tile - 1))
                    act.sem_inc(act_waited, 1)
                    n = KW if layer == 0 else LK
                    act.activation(k[t % 2][0][:, 0:n], ps_k[:, 0:n], ACT.Identity,
                                   bias=cols(att)[:, ds(place.column((C_BK0, C_BK1), t), 1)]).then_inc(k_hi, 1)

                def value(place, i):
                    n = KEY_TILES[i][1]
                    act.wait_ge(v_mm, 3 * place.batch + i + 1)
                    wait(act, av_mm, att.units_before(place.tile - NT))
                    act.activation(v[place.parity][0:n, i, :], ps_v[0:n, :], ACT.Identity).then_inc(v_ev, 1)

                def turned(place, t, j):
                    unit, buf = place.unit + sub * t + j, (j if layer == 0 else t) % 2
                    act.wait_ge(t_mm, unit + 1)
                    wait(act, av_mm, unit - 1)
                    act.activation(prob_t[buf][:], ps_t[buf][:, 0:3 * LQ], ACT.Identity).then_inc(t_ev, 1)

                def exp(place, t, j):
                    unit, buf = place.unit + sub * t + j, (j if layer == 0 else t) % 2
                    act.wait_ge(s_max, unit + 1)
                    wait(act, t_mm, unit - 1)
                    src = ps_s[buf] if layer else prob[buf]
                    act.activation(prob[buf][0:LQ, 0:att.keys], src[0:LQ, 0:att.keys], ACT.Exp,
                                   bias=max_neg[0:LQ, buf:buf + 1],
                                   accum_out=prob_sum[0:LQ, buf:buf + 1]).then_inc(s_exp, 1)

                def output(place):
                    act.wait_ge(av_mm, att.units_before(place.tile + NT))
                    wait(act, o_lo, place.batch)
                    act.sem_inc(act_waited, 1)
                    for t in range(NT):
                        act.activation(o[:, t * LQ:(t + 1) * LQ], ps_o[place.parity][:, t * LQ:(t + 1) * LQ],
                                       ACT.Identity, bias=cols(att)[:, ds(place.column((C_BV0, C_BV1), t), 1)])\
                            .then_inc(o_ev, 1)

                def prologue(place):
                    for i in range(3):
                        value(place, i)
                    key_hi(place, 0)
                    key_hi(place, 1)
                    exp(place, 0, 0)
                    if layer == 1:
                        key_hi(place, 2)
                    exp(*place.at(0, 0, 1))
                    turned(place, 0, 0)

                def one_batch(place):
                    for t in range(NT):
                        for j in range(sub):
                            if place.at(t, j, 1):
                                turned(*place.at(t, j, 1))
                            if place.at(t, j, 2):
                                exp(*place.at(t, j, 2))
                            if place.swap and j == sub - 1:
                                split_hi(0, place.block_a + 1, [t], lambda s: (k_mm, place.tile + s + 1))
                            if j == att.key_slot and place.key(t + att.key_ahead):
                                key_hi(*place.key(t + att.key_ahead))
                            if (t, j) in V_SLOTS[layer] and not place.final:
                                value(place.next(), V_SLOTS[layer][t, j])
                            if place.swap and (t, j) == (0, 0):
                                split_hi(1, place.block_b + 1, range(4), lambda s: (v_mm, 3 * place.batch + 3))
                    output(place)

                batches(act, att, a, prologue, one_batch)

            def project(layer, a, group, slot, n, step, x0):
                split_hi(slot, n + 1, range(4), lambda s: (y_mm, x0 + RT))

            def mlp(m, fg, e, x0):
                na, nb = mlp_block(m, fg)
                for c, (r0, nr) in enumerate(MLP_CHUNKS):
                    for f in range(4):
                        u = 12 * (4 * m + fg) + 4 * c + f
                        col = (C_FC0, C_FC1)[m] + 4 * fg + f
                        act.wait_ge(h_mm, u + 1)
                        wait(act, h_lo, u - 1)
                        act.sem_inc(act_waited, 1)
                        act.activation(prob[f % 2][:, 0:nr], ps_s[f % 2][:, 0:nr],
                                       ACT.Gelu if m else ACT.Gelu_apprx_tanh,
                                       bias=col_a[:, ds(col, 1)]).then_inc(h_act, 1)
                split_hi(0, na + 1, range(4), lambda s: (h_mm, 12 * (4 * m + fg) + 8 + s + 1))
                split_hi(1, nb + 1, range(4), lambda s: (y_mm, x0 + RT))

            split_hi(0, 0, range(4), None)
            split_hi(1, 0, range(4), None)
            act.wait_ge(vec_ev, 4)
            schedule(act, ln, query, attend, project, mlp)

        @block.vector
        def _(dve):
            def split_lo(slot, n, subs):
                if not exists(slot, n):
                    return
                for s in subs:
                    dve.wait_ge(w_hi[slot], 4 * n + s + 1)
                    part = slice(s * P, (s + 1) * P)
                    dve.tensor_tensor(w[slot][1][:, :, part], w_raw[slot][:, :, part], w[slot][0][:, :, part],
                                      ALU.subtract).then_inc(w_lo[slot], 1)

            def ln(e, x0):
                for r in range(RT):
                    if isinstance(e, int) and e == 0:
                        dve.wait_ge(start_in, 16)
                    else:
                        dve.wait_ge(x_add, x0 - RT + r + 1)
                    dve.bn_stats(stats[:, r, :], x[:, r, :]).then_inc(ln_stat, 1)
                dve.wait_ge(ln_stat, RT * e + RT)
                dve.sem_inc(dve_waited, 1)
                for r in range(RT):
                    dve.bn_aggr(mean_var[:, r, :], stats[:, r, :]).then_inc(ln_agg, 1)
                dve.wait_ge(ln_agg, RT * e + RT)
                dve.tensor_scalar(var_eps[:], mean_var[:, :, 1], EPS, None, ALU.add).then_inc(ln_eps, 1)
                dve.wait_ge(ln_std, e + 1)
                dve.reciprocal(rstd[:], std[:]).then_inc(ln_rstd, 1)
                dve.wait_ge(ln_rstd, e + 1)

                def normalized(r):
                    wait(dve, ln_turn, RT * e + r - 1)
                    dve.tensor_scalar(prob[r % 2][:], x[:, r, :], mean_var[:, r, 0:1], rstd[:, r:r + 1],
                                      ALU.subtract, ALU.mult).then_inc(ln_xhat, 1)

                normalized(0)
                for r in range(RT):
                    if r + 1 < RT:
                        normalized(r + 1)
                    z = o[:].rearrange("p (k n) -> p k n", k=DT)
                    dve.wait_ge(ln_act, RT * e + r + 1)
                    dve.tensor_copy(act_t[0][:, :, r * P:(r + 1) * P], z).then_inc(ln_hi, 1)
                    dve.wait_ge(ln_hi, RT * e + r + 1)
                    dve.tensor_tensor(act_t[1][:, :, r * P:(r + 1) * P], z, act_t[0][:, :, r * P:(r + 1) * P],
                                      ALU.subtract).then_inc(ln_lo, 1)

            def query(layer, a, group, slot, n, step):
                for i in range(2 * NT):
                    t, half = i // 2, i % 2
                    hi, lo = (cs[half][s][:, 0:HALF] for s in range(2))
                    dve.wait_ge(q_act, 8 * step + i + 1)
                    wait(dve, q_out[half], 32 * (4 * step + t))
                    dve.tensor_copy(hi, prob[half][:, 0:HALF]).then_inc(q_hi, 1)
                    dve.wait_ge(q_hi, 8 * step + i + 1)
                    dve.tensor_tensor(lo, prob[half][:, 0:HALF], hi, ALU.subtract).then_inc(q_lo, 1)
                split_lo(slot, n + 1, range(4))

            def attend(att, a):
                sub, layer = att.sub, att.layer

                def context_hi(place):
                    wait(dve, k_mm, place.tile - NT)
                    dve.tensor_copy(cs[place.parity][0][:, 0:DT * KW].rearrange("p (k n) -> p k n", k=DT),
                                    ctx_t[:, :, ds(place.b * KW, KW)]).then_inc(cs_hi, 1)

                def key_lo(place, t):
                    n = KW if layer == 0 else LK
                    dve.wait_ge(k_hi, place.tile + t + 1)
                    dve.scalar_tensor_tensor(out=k[t % 2][1][:, 0:n], in0=ps_k[:, 0:n],
                                             scalar=cols(att)[:, ds(place.column((C_BK0, C_BK1), t), 1)],
                                             in1=k[t % 2][0][:, 0:n], op0=ALU.add, op1=ALU.subtract).then_inc(k_lo, 1)

                def key_caps(place):
                    dve.tensor_scalar(key_cap[:], mask_u8[:, ds(place.b * LK, LK)], -0.5, LARGEST,
                                      ALU.add, ALU.mult).then_inc(cap_half, 1)
                    dve.wait_ge(cap_half, place.batch + 1)
                    dve.tensor_scalar(key_cap[:], key_cap[:], 2.0, None, ALU.mult).then_inc(cap_full, 1)
                    dve.wait_ge(cap_full, place.batch + 1)

                def maximum(place, t, j):
                    unit, buf = place.unit + sub * t + j, (j if layer == 0 else t) % 2
                    dve.wait_ge(s_mm, unit + 1)
                    neg = max_neg[0:LQ, buf:buf + 1]
                    if layer:
                        dve.tensor_reduce(neg, ps_s[buf][0:LQ, 0:KW], AX_X, ALU.max, negate=True).then_inc(s_max, 1)
                        return
                    if (t, j) == (0, 0):
                        key_caps(place)
                    masked = prob[buf][0:LQ, 0:LK]
                    wait(dve, t_mm, unit - 1)
                    dve.tensor_tensor(masked, ps_s[buf][0:LQ, 0:LK], key_cap[:], ALU.min).then_inc(s_cap, 1)
                    dve.wait_ge(s_cap, unit + 1)
                    dve.tensor_reduce(neg, masked, AX_X, ALU.max, negate=True).then_inc(s_max, 1)

                def normalize(place, t, j):
                    unit, buf = place.unit + sub * t + j, (j if layer == 0 else t) % 2
                    dve.wait_ge(s_exp, unit + 1)
                    dve.reciprocal(prob_rcp[0:LQ, buf:buf + 1], prob_sum[0:LQ, buf:buf + 1]).then_inc(s_rcp, 1)
                    dve.wait_ge(s_rcp, unit + 1)
                    dve.tensor_scalar(prob[buf][0:LQ, 0:att.keys], prob[buf][0:LQ, 0:att.keys],
                                      prob_rcp[0:LQ, buf:buf + 1], None, ALU.mult).then_inc(s_norm, 1)

                def output(place):
                    dve.wait_ge(o_ev, NT * place.batch + NT)
                    wait(dve, o_out, 32 * place.batch)
                    dve.tensor_copy(o_split[0][:], o[:, 0:NT * LQ]).then_inc(o_hi, 1)
                    dve.wait_ge(o_hi, place.batch + 1)
                    dve.tensor_tensor(o_split[1][:], o[:, 0:NT * LQ], o_split[0][:], ALU.subtract).then_inc(o_lo, 1)

                def prologue(place):
                    if layer == 0:
                        dve.wait_ge(ctx_in_sem, 16)
                    for half in range(2):
                        dve.wait_ge(q_out[half], 32 * NT * (1 + 4 * (a + 1) if layer else 1))
                    context_hi(place)
                    context_hi(place.next())
                    key_lo(place, 0)
                    key_lo(place, 1)
                    maximum(place, 0, 0)
                    if layer == 0:
                        maximum(place, 0, 1)
                    normalize(place, 0, 0)
                    if layer == 1:
                        key_lo(place, 2)
                        maximum(place, 1, 0)
                    normalize(*place.at(0, 0, 1))
                    if layer == 0:
                        maximum(place, 0, 2)

                def one_batch(place):
                    for t in range(NT):
                        for j in range(sub):
                            if layer == 1 and place.at(t, j, 2):
                                maximum(*place.at(t, j, 2))
                            if place.at(t, j, 2):
                                normalize(*place.at(t, j, 2))
                            if layer == 0 and place.at(t, j, 3):
                                maximum(*place.at(t, j, 3))
                            if place.swap and j == sub - 1:
                                split_lo(0, place.block_a + 1, [t])
                            if j == att.key_slot and place.key(t + att.key_ahead):
                                key_lo(*place.key(t + att.key_ahead))
                            if (t, j) == att.context_slot and place.after(2):
                                context_hi(place.after(2))
                            if place.swap and (t, j) == (0, 0):
                                split_lo(1, place.block_b + 1, range(4))
                    output(place)

                batches(dve, att, a, prologue, one_batch)

            def add_y(r, e, x0):
                dve.wait_ge(y_mm, x0 + r + 1)
                dve.wait_ge(bias_add, RT * e + r + 1)
                wait(dve, x_add, x0 + r + 1 - RT)
                dve.tensor_tensor(x[:, r, :], ps_y[r % 2][:], x[:, r, :], ALU.add).then_inc(x_add, 1)

            def project(layer, a, group, slot, n, step, x0):
                for r in range(RT):
                    add_y(r, 2 + a if layer else 0, x0)
                split_lo(slot, n + 1, range(4))

            def mlp(m, fg, e, x0):
                na, nb = mlp_block(m, fg)

                def hidden(c):
                    r0, nr = MLP_CHUNKS[c]
                    wait(dve, y_mm, x0 + MLP_CHUNKS[0][1] // P if c == 2 else x0)
                    for f in range(4):
                        u = 12 * (4 * m + fg) + 4 * c + f
                        hi, lo = (cs[c % 2][s][:, f * CHUNK_MAX:f * CHUNK_MAX + nr] for s in range(2))
                        dve.wait_ge(h_act, u + 1)
                        dve.tensor_copy(hi, prob[f % 2][:, 0:nr]).then_inc(h_hi, 1)
                        dve.wait_ge(h_hi, u + 1)
                        dve.tensor_tensor(lo, prob[f % 2][:, 0:nr], hi, ALU.subtract).then_inc(h_lo, 1)

                def add_chunk(c):
                    r0, nr = MLP_CHUNKS[c]
                    for r in range(r0 // P, (r0 + nr) // P):
                        add_y(r, e, x0)

                hidden(0)
                hidden(1)
                add_chunk(0)
                hidden(2)
                split_lo(0, na + 1, range(4))
                add_chunk(1)
                add_chunk(2)
                split_lo(1, nb + 1, range(4))

            for i in range(2):
                last = dve.memset(ps_t[i][:], 0.0)
            last.then_inc(cleared, 1)
            dve.wait_ge(vec_t, 1)
            dve.wait_ge(cleared, 1)
            dve.tensor_scalar(col_a[:, 0:NT], ps_t[0][:, 0:NT], float(HD0 ** -0.5), None, ALU.mult).then_inc(vec_ev, 1)
            dve.tensor_copy(col_a[:, NT:N_CA], ps_t[0][:, NT:N_CA]).then_inc(vec_ev, 1)
            by_layer = [t.rearrange("p (a c) -> p a c", a=2) for t in (col_b[:], ps_t[1][:, 0:P])]
            dve.tensor_scalar(by_layer[0][:, :, 0:16], by_layer[1][:, :, 0:16], float(HD1 ** -0.5), None,
                              ALU.mult).then_inc(vec_ev, 1)
            dve.tensor_copy(by_layer[0][:, :, 16:N_CB1], by_layer[1][:, :, 16:N_CB1]).then_inc(vec_ev, 1)
            dve.wait_ge(vec_ev, 4)
            extra = [t.rearrange("p (a c) -> p a c", a=2) for t in (xk[0][:], xk[1][:])]
            dve.tensor_copy(extra[0], by_layer[0][:, :, C_XK1:N_CB1]).then_inc(vec_split, 1)
            dve.wait_ge(vec_split, 1)
            dve.tensor_tensor(extra[1], by_layer[0][:, :, C_XK1:N_CB1], extra[0], ALU.subtract).then_inc(vec_split, 1)
            dve.wait_ge(vecs_in, 16 * 6)
            dve.tensor_tensor(key_cap[0:32, 0:P], prob[0][0:32, 2 * P:3 * P], prob[0][0:32, 3 * P:4 * P],
                              ALU.subtract).then_inc(xv_diff, 1)
            split_lo(0, 0, range(4))
            split_lo(1, 0, range(4))
            dve.wait_ge(xv_out, 16)
            dve.wait_ge(xv_diff, 1)
            schedule(dve, ln, query, attend, project, mlp)

        @block.tensor
        def _(pe):
            def product(out, stationary, moving, first, last):
                (w_h, w_l), (m_h, m_l) = stationary, moving
                pe.matmul(out, w_h, m_h, start=first, stop=False)
                pe.matmul(out, w_h, m_l, start=False, stop=False)
                return pe.matmul(out, w_l, m_h, start=False, stop=last)

            def ln(e, x0):
                for r in range(RT):
                    pe.wait_ge(ln_xhat, RT * e + r + 1)
                    wait(pe, ln_act, RT * e + r - 1)
                    if isinstance(e, int) and e == 0:
                        pe.wait_ge(vec_ev, 4)
                    for c in range(DT):
                        last = pe.transpose(ps_t[r % 2][:, c * P:(c + 1) * P], prob[r % 2][:, c * P:(c + 1) * P], ident[:])
                    last.then_inc(ln_turn, 1)

            def query(layer, a, group, slot, n, step):
                pe.wait_ge(ln_lo, RT * (2 + a if layer else 0) + RT)
                for i in range(2 * NT):
                    t, half = i // 2, i % 2
                    pe.wait_ge(w_lo[slot], 4 * n + t + 1)
                    wait(pe, q_act, 8 * step + i - 1)
                    for c in range(DT):
                        last = product(ps_y[half][:, 0:HALF],
                                       [w[slot][s][:, c, t * P:(t + 1) * P] for s in range(2)],
                                       [act_t[s][:, c, half * HALF:(half + 1) * HALF] for s in range(2)],
                                       c == 0, c == DT - 1)
                    last.then_inc(q_mm, 1)

            def attend(att, a):
                sub, layer = att.sub, att.layer

                def context_ready(place):
                    pe.wait_ge(cs_hi, place.batch + 1)
                    pe.wait_ge(cs_lo, place.batch + 1)

                def key(place, t):
                    tile = place.tile + t
                    if t == 0:
                        context_ready(place)
                    pe.wait_ge(w_lo[0], 4 * place.block_a + t + 1)
                    wait(pe, k_lo, tile)
                    for c in range(DT):
                        last = product(ps_k[:, 0:KW],
                                       [w[0][s][:, c, t * P:(t + 1) * P] for s in range(2)],
                                       [cs[place.parity][s][:, c * KW:(c + 1) * KW] for s in range(2)],
                                       c == 0, c == DT - 1)
                    last.then_inc(k_mm, 1)

                def value(place, i):
                    if i == 0:
                        context_ready(place)
                        pe.wait_ge(w_lo[1], 4 * place.block_b + 4)
                    wait(pe, v_ev, 3 * place.batch + i)
                    k0, n = KEY_TILES[i]
                    for c in range(DT):
                        last = product(ps_v[0:n, :],
                                       [cs[place.parity][s][:, c * KW + k0:c * KW + k0 + n] for s in range(2)],
                                       [w[1][s][:, c, :] for s in range(2)], c == 0, c == DT - 1)
                    last.then_inc(v_mm, 1)

                def scores(place, t, j):
                    unit, buf = place.unit + sub * t + j, (j if layer == 0 else t) % 2
                    if j == 0:
                        pe.wait_ge(k_lo, place.tile + t + 1)
                        if layer:
                            pe.wait_ge(k_extra, place.tile + t + 1 - att.tile0)
                    if (t, j) == (0, 0):
                        pe.wait_ge(q_in[place.parity], 32 * place.same_parity + 32)
                    wait(pe, s_exp if layer else s_cap, unit - 1)
                    rows = slice(0, P) if layer else slice(HD0 * j, HD0 * (j + 1))
                    product(ps_s[buf][0:LQ, 0:KW],
                            [q[place.parity][s][rows, t * LQ:(t + 1) * LQ] for s in range(2)],
                            [k[t % 2][s][rows, :] for s in range(2)], True, True).then_inc(s_mm, 1)

                def turn(place, t, j):
                    unit, buf = place.unit + sub * t + j, (j if layer == 0 else t) % 2
                    pe.wait_ge(s_norm, unit + 1)
                    wait(pe, t_ev, unit - 1)
                    for i, n in enumerate(att.vals()):
                        last = pe.transpose(ps_t[buf][0:n, i * LQ:(i + 1) * LQ],
                                            prob[buf][0:LQ, i * P:i * P + n], ident[0:LQ, 0:LQ])
                    last.then_inc(t_mm, 1)

                def weighted(place, t, j):
                    unit, buf = place.unit + sub * t + j, (j if layer == 0 else t) % 2
                    if (t, j) == (0, 0):
                        pe.wait_ge(v_ev, 3 * place.batch + 3)
                        if layer:
                            pe.wait_ge(xv_in[place.parity], 16 * place.block + 16)
                        wait(pe, o_ev, NT * (place.batch - 1))
                    pe.wait_ge(t_ev, unit + 1)
                    rows = slice(0, P) if layer else slice(HD0 * j, HD0 * (j + 1))
                    for i, n in enumerate(att.vals()):
                        last = pe.matmul(ps_o[place.parity][rows, t * LQ:(t + 1) * LQ],
                                         v[place.parity][0:n, i, t * P + rows.start:t * P + rows.stop],
                                         prob_t[buf][0:n, i * LQ:(i + 1) * LQ], start=(i == 0), stop=(i == 2))
                    last.then_inc(av_mm, 1)

                def prologue(place):
                    pe.wait_ge(q_act, 8 * (1 + 4 * (a + 1) if layer else 1))
                    for i in range(3):
                        value(place, i)
                    key(place, 0)
                    key(place, 1)
                    scores(place, 0, 0)
                    if layer == 1:
                        key(place, 2)
                    for unit in range(1, att.score_ahead):
                        scores(*place.at(0, 0, unit))
                    turn(place, 0, 0)

                def one_batch(place):
                    for t in range(NT):
                        for j in range(sub):
                            if place.at(t, j, 1):
                                turn(*place.at(t, j, 1))
                            if place.at(t, j, att.score_ahead):
                                scores(*place.at(t, j, att.score_ahead))
                            if j == att.key_slot and place.key(t + att.key_ahead):
                                key(*place.key(t + att.key_ahead))
                            weighted(place, t, j)
                            if (t, j) in V_SLOTS[layer] and not place.final:
                                value(place.next(), V_SLOTS[layer][t, j])

                batches(pe, att, a, prologue, one_batch)

            def bank_read(r, x0):
                wait(pe, x_add, x0 + r - 1 if r else x0)

            def project(layer, a, group, slot, n, step, x0):
                pe.wait_ge(w_lo[slot], 4 * n + 4)
                for c, (r0, nr) in enumerate(OUT_CHUNKS):
                    pe.wait_ge(o_in[c], 32 * step + 32)
                    for r in range(r0, r0 + nr):
                        bank_read(r, x0)
                        for t in range(NT):
                            last = product(ps_y[r % 2][:], [act_t[s][:, t, r * P:(r + 1) * P] for s in range(2)],
                                           [w[slot][s][:, t, :] for s in range(2)], t == 0, t == NT - 1)
                        last.then_inc(y_mm, 1)

            def mlp(m, fg, e, x0):
                na, nb = mlp_block(m, fg)

                def up(c):
                    r0, nr = MLP_CHUNKS[c]
                    for f in range(4):
                        u = 12 * (4 * m + fg) + 4 * c + f
                        pe.wait_ge(w_lo[0], 4 * na + f + 1)
                        wait(pe, h_act, u - 1)
                        for t in range(DT):
                            last = product(ps_s[f % 2][:, 0:nr], [w[0][s][:, t, f * P:(f + 1) * P] for s in range(2)],
                                           [act_t[s][:, t, r0:r0 + nr] for s in range(2)], t == 0, t == DT - 1)
                        last.then_inc(h_mm, 1)

                def down(c):
                    r0, nr = MLP_CHUNKS[c]
                    pe.wait_ge(h_lo, 12 * (4 * m + fg) + 4 * c + 4)
                    pe.wait_ge(w_lo[1], 4 * nb + 4)
                    for i in range(nr // P):
                        r = r0 // P + i
                        bank_read(r, x0)
                        for f in range(4):
                            at = f * CHUNK_MAX + i * P
                            last = product(ps_y[r % 2][:], [cs[c % 2][s][:, at:at + P] for s in range(2)],
                                           [w[1][s][:, f, :] for s in range(2)], f == 0, f == 3)
                        last.then_inc(y_mm, 1)

                pe.wait_ge(ln_lo, RT * e + RT)
                up(0)
                up(1)
                down(0)
                up(2)
                down(1)
                down(2)

            pe.wait_ge(vecs_in, 16 * 6)
            pe.wait_ge(cleared, 1)
            pe.transpose(ps_t[0][:, 0:N_CA], prob[0][0:N_CA, 0:P], ident[0:N_CA, 0:N_CA])
            pe.transpose(ps_t[1][:, 0:P], prob[0][:, P:2 * P], ident[:]).then_inc(vec_t, 1)
            schedule(pe, ln, query, attend, project, mlp)


def kernel(**inputs):
    import numpy as np
    import concourse.bacc as bacc
    from concourse.bass_utils import run_bass_kernel_spmd

    g = {name: np.asarray(value) for name, value in inputs.items()}
    l0, l1 = (lambda n: g["L0_xattn_" + n]), (lambda n: g["L1_xattn_" + n])

    def blocks(weight):
        rows, columns = weight.shape
        if rows == D:
            b = weight.reshape(DT, P, columns // D, D).transpose(2, 1, 0, 3)
        else:
            b = weight.reshape(rows // D, DT, P, D).transpose(0, 2, 1, 3)
        return list(b.reshape(-1, P, DT * D))

    a = blocks(l0("q_w")) + blocks(l0("k_w")) + blocks(l0("cproj_w")) + blocks(l0("fc_w"))
    b = blocks(l0("v_w")) + blocks(l0("proj_w"))
    for i in "12":
        wq, wk, wv, wo = (blocks(l1(f"w{m}{i}")) for m in "qkvo")
        a += wq[0::2] + wk + wo[0::2]
        b += wq[1::2] + wv + wo[1::2]
    a += blocks(l1("w_fc1"))
    b += blocks(l1("w_fc2"))
    blocks_a, blocks_b = np.stack(a), np.stack(b)

    def rows(*names):
        return np.concatenate([g[n].reshape(-1, P) for n in names])

    vec_a = rows("L0_xattn_q_b", "L0_xattn_k_b", "L0_xattn_v_b", "L0_xattn_fc_b", "L1_xattn_b_fc1",
                 "L0_xattn_ln1_w", "L0_xattn_ln1_b", "L0_xattn_ln2_w", "L0_xattn_ln2_b",
                 "L1_xattn_ln1_scale", "L1_xattn_ln1_offset", "L1_xattn_ln2_scale", "L1_xattn_ln2_offset",
                 "L1_xattn_ln_mlp_scale", "L1_xattn_ln_mlp_offset")
    vec_b = rows(*(f"L1_xattn_{n}{i}" for i in "12" for n in ("bq", "bk", "bv", "bias_k")))
    ctx = np.zeros((P, DT, NB, KW), g["ctx_2048"].dtype)
    ctx[:, :, :, 0:LK] = g["ctx_2048"].transpose(2, 0, 1).reshape(DT, P, NB, LK).transpose(1, 0, 2, 3)
    arrays = {
        "x": g["x"].reshape(ROWS, D),
        "ctx_t": ctx.reshape(P, DT * NB * KW),
        "mask": g["mask_BxS2_bf1"].reshape(1, NB * LK).view(np.uint8),
        "blocks_a": blocks_a, "blocks_b": blocks_b, "vec_a": vec_a, "vec_b": vec_b,
        "value_rows": rows("L1_xattn_bias_v1", "L1_xattn_bias_v2"),
        "value_bias_rows": rows("L1_xattn_bv1", "L1_xattn_bv2"),
        "row_bias": np.stack([l0("cproj_b"), l0("proj_b"), l1("bo1"), l1("bo2"), l1("b_fc2")]),
        "eye": np.eye(P, dtype=np.float32),
    }
    nc = bacc.Bacc("TRN2", target_bir_lowering=False, num_devices=1)
    arrays = {f"in_{n}": np.ascontiguousarray(v) for n, v in arrays.items()}
    args = [nc.dram_tensor(n, v.shape, mybir.dt.from_np(v.dtype), kind="ExternalInput").ap() for n, v in arrays.items()]
    out = nc.dram_tensor("out", (ROWS, D), F32, kind="ExternalOutput").ap()
    build(nc, *args, out)
    result = run_bass_kernel_spmd(nc, [arrays], core_ids=[0])
    return result.results[0]["out"].reshape(NB, LQ, D)
```

```python
from contextlib import ExitStack

import concourse.bass as bass
from concourse import mybir

F32 = mybir.dt.float32
F32R = mybir.dt.float32r
U8 = mybir.dt.uint8
ACT = mybir.ActivationFunctionType
ALU = mybir.AluOpType
AX_X = mybir.AxisListType.X
ds = bass.ds

P = 128
NB = 8
LQ = 112
LK = 375
KW = LK + 1
D = 512
DT = D // P
ROWS = NB * LQ
RT = ROWS // P
HALF = ROWS // 2
KEY_TILES = [(0, 128), (128, 128), (256, LK - 256)]
GROUPS = 4
PAIRS = NB // 2
NT = 4
SUB0 = 4
HD0, HD1 = 32, 128
EPS = 1e-5
LARGEST = 3.4028234663852886e38

A_Q0, A_K0, A_O0, A_M0 = 0, 1, 2, 3
B_V0, B_M0 = 0, 1
A_L1, B_L1, PER_LAYER = 7, 5, 8
A_M1, B_M1 = A_L1 + 2 * PER_LAYER, B_L1 + 2 * PER_LAYER
N_A, N_B = A_M1 + 4, B_M1 + 4

C_BQ0, C_BK0, C_BV0, C_FC0, C_FC1, C_LN = 0, 4, 8, 12, 28, 44
N_CA = C_LN + 8 * 5
C_BQ1, C_BK1, C_BV1, C_XK1, N_CB1 = 0, 16, 32, 48, 64

OUT_CHUNKS = [(0, 3), (3, 3), (6, 2)]
CHUNK_FREE = [-(-(b0 + nb) * LQ // P) for b0, nb in OUT_CHUNKS]
CHUNK_OF = [min(c for c, (b0, nb) in enumerate(OUT_CHUNKS) if (r + 1) * P <= (b0 + nb) * LQ) for r in range(RT)]
MLP_CHUNKS = [(0, 384), (384, 256), (640, 256)]
CHUNK_MAX = 384


class Attention:

    def __init__(self, layer, sub, tile0, unit0, batch0):
        self.layer, self.sub = layer, sub
        self.tile0, self.unit0, self.batch0 = tile0, unit0, batch0
        self.score_ahead = 3 if layer == 0 else 2
        self.key_ahead = 2 if layer == 0 else 3
        self.key_parts = {2: (0, 2), 3: (2, DT)} if layer == 0 else {0: (0, DT)}
        self.key_slot = max(self.key_parts)
        self.split_slots = {(NB - 1, t): t for t in range(NT)} if layer == 0 else {
            (NB - 2, 2): 0, (NB - 2, 3): 1, (NB - 1, 0): 2, (NB - 1, 1): 3}
        if layer == 0:
            late = {(t, j): ([], [(t - 1, 2 * j, 2 * j + 2)]) for t in range(1, NT) for j in range(2)}
        else:
            late = {(t, 0): ([], [(t - 1, 0, DT)]) for t in range(1, NT)}
        even = {(0, 0): ([], [(0, 0, 3)]), (1, 0): ([(0, 3, DT)], [(1, 0, 2)]),
                (2, 0): ([(1, 2, DT)], [(2, 0, 1)]), (3, 0): ([(2, 1, DT)], [])}
        self.value_parts = {True: late, False: even if layer == 1 else late}
        self.context_slot = (2, 0) if layer == 0 else (1, 0)
        self.keys = LK if layer == 0 else KW

    def units_before(self, tile):
        return self.unit0 + self.sub * (tile - self.tile0)

    def vals(self):
        return [n if i < 2 else n + self.layer for i, (_, n) in enumerate(KEY_TILES)]


class Place:

    def __init__(self, att, a, group, pair, parity, final=False):
        self.att, self.a, self.group, self.pair, self.parity = att, a, group, pair, parity
        self.b = 2 * pair + parity
        self.swap = isinstance(self.b, int) and self.b == NB - 1
        self.last_block = att.layer == 1 and isinstance(group, int) and group == GROUPS - 1
        self.first = NB * a + self.b
        self.final_pair = final
        self.final = final and self.swap
        blocks = a * GROUPS + group
        self.batch = att.batch0 + blocks * NB + self.b
        self.same_parity = att.batch0 // 2 + blocks * PAIRS + pair
        self.block = blocks
        self.tile = self.batch * NT
        self.unit = att.units_before(self.tile)
        self.stores = blocks * PAIRS + pair
        self.block_a = A_K0 if att.layer == 0 else A_L1 + 2 + PER_LAYER * a + group
        self.block_b = B_V0 if att.layer == 0 else B_L1 + 2 + PER_LAYER * a + group

    def next(self):
        if self.swap:
            return Place(self.att, self.a, self.group + 1, 0, 0)
        if self.parity:
            return Place(self.att, self.a, self.group, self.pair + 1, 0, self.final_pair)
        return Place(self.att, self.a, self.group, self.pair, 1, self.final_pair)

    def key(self, t):
        if t < NT:
            return self, t
        return None if self.final else (self.next(), t - NT)

    def at(self, t, j, ahead):
        n = self.att.sub * t + j + ahead
        tile = self.key(n // self.att.sub)
        return tile and (*tile, n % self.att.sub)

    def after(self, batches):
        if batches == 0:
            return self
        return None if self.final else self.next().after(batches - 1)

    def split_column(self, t):
        return self.att.split_slots.get((self.b, t)) if isinstance(self.b, int) else None

    def column(self, kind, t):
        if self.att.layer == 0:
            return kind[0] + t
        return N_CB1 * self.a + kind[1] + NT * self.group + t


ATT0 = Attention(0, SUB0, 0, 0, 0)
ATT1 = Attention(1, 1, NB * NT, NB * NT * SUB0, NB)


def wait(eng, sem, value):
    if isinstance(value, int) and value <= 0:
        return
    eng.wait_ge(sem, value)


def build(nc, x_in, ctx_in, mask_in, blocks_a, blocks_b, vec_a, vec_b, value_rows, value_bias_rows, row_bias, eye, out):
    q_scr = [nc.dram_tensor(f"q_{s}_scratch", [GROUPS, NB, P, NT * LQ], F32).ap() for s in ("hi", "lo")]
    o_scr = nc.dram_tensor("o_scratch", [GROUPS, NB, P, NT * LQ], F32).ap()
    xv_scr = nc.dram_tensor("extra_value_scratch", [2, GROUPS, D], F32).ap()

    with ExitStack() as ctx:
        def sb(name, shape, dt=F32):
            return ctx.enter_context(nc.sbuf_tensor(name, shape, dt))

        def sem(name):
            return ctx.enter_context(nc.semaphore(name))

        ctx_t = sb("ctx_t", [P, DT, NB * KW])
        x = sb("x", [P, RT, D])
        ident = sb("ident", [P, P])
        col_a = sb("col_a", [P, N_CA])
        col_b = sb("col_b", [P, 2 * N_CB1])
        xk = [sb(f"xk_{s}", [P, 32], F32R) for s in ("hi", "lo")]
        bias_row = sb("bias_row", [P, D])
        mask_u8 = sb("mask_u8", [LQ, NB * LK], U8)
        key_cap = sb("key_cap", [LQ, LK])
        act_t = [sb(f"act_t_{s}", [P, DT, ROWS], F32R) for s in ("hi", "lo")]
        w_raw = [sb(f"w_raw_{s}", [P, DT, D]) for s in "ab"]
        w = [[sb(f"w_{s}_{h}", [P, DT, D], F32R) for h in ("hi", "lo")] for s in "ab"]
        cs = [[sb(f"cs{i}_{h}", [P, DT * CHUNK_MAX], F32R) for h in ("hi", "lo")] for i in range(2)]
        q = [[sb(f"q{i}_{h}", [P, NT * LQ], F32R) for h in ("hi", "lo")] for i in range(2)]
        v = [sb(f"v{i}", [P, 3, D]) for i in range(2)]
        k = [[sb(f"k{i}_{h}", [P, KW], F32R) for h in ("hi", "lo")] for i in range(2)]
        prob = [sb(f"prob{i}", [P, D]) for i in range(2)]
        prob_t = [sb(f"prob_t{i}", [P, 3 * LQ]) for i in range(2)]
        o = [sb(f"o{i}", [P, D]) for i in range(2)]
        stats = sb("stats", [P, RT, 6])
        mean_var = sb("mean_var", [P, RT, 2])
        var_eps = sb("var_eps", [P, RT])
        std = sb("std", [P, RT])
        rstd = sb("rstd", [P, RT])
        max_neg = sb("max_neg", [P, 2])
        prob_sum = sb("prob_sum", [P, 2])
        prob_rcp = sb("prob_rcp", [P, 2])

        def bank(name):
            return ctx.enter_context(nc.psum_tensor(name, [P, 512], F32))

        ps_k, ps_v = bank("ps_k"), bank("ps_v")
        ps_s = [bank(f"ps_s{i}") for i in range(2)]
        ps_t = [bank(f"ps_t{i}") for i in range(2)]
        ps_o = [bank(f"ps_o{i}") for i in range(2)]
        ps_y = [ps_k, ps_v]

        start_in, vecs_in = sem("start_in"), sem("vecs_in")
        ctx_in_sem = [sem("ctx_in_first_pair"), sem("ctx_in_others")]
        vec_t, vec_ev, vec_split, xv_diff, xv_out = (sem(n) for n in ("vec_t", "vec_ev", "vec_split", "xv_diff", "xv_out"))
        cleared = sem("cleared")
        w_in = [sem(f"w_in_{s}") for s in "ab"]
        w_hi = [sem(f"w_hi_{s}") for s in "ab"]
        w_lo = [sem(f"w_lo_{s}") for s in "ab"]
        ln_stat, ln_agg, ln_eps, ln_std, ln_rstd, ln_xhat, ln_turn, ln_act, ln_hi, ln_lo = (
            sem("ln_" + n) for n in ("stat", "agg", "eps", "std", "rstd", "xhat", "turn", "act", "hi", "lo"))
        bias_in, bias_add = sem("bias_in"), sem("bias_add")
        q_mm, q_act, q_hi, q_lo = (sem("q_" + n) for n in ("mm", "act", "hi", "lo"))
        q_out = [sem(f"q_out{i}") for i in range(2)]
        q_in = [sem(f"q_in{i}") for i in range(2)]
        cs_hi, cs_lo = sem("cs_hi"), sem("cs_lo")
        k_mm, k_hi, k_lo, k_extra = sem("k_mm"), sem("k_hi"), sem("k_lo"), sem("k_extra")
        v_mm, v_ev = sem("v_mm"), sem("v_ev")
        xv_in = [sem(f"xv_in{i}") for i in range(2)]
        s_mm, s_cap, s_max, s_exp, s_rcp, s_norm = (
            sem("s_" + n) for n in ("mm", "cap", "max", "exp", "rcp", "norm"))
        cap_half, cap_full = sem("cap_half"), sem("cap_full")
        t_mm, t_ev, av_mm = sem("t_mm"), sem("t_ev"), sem("av_mm")
        o_ev, o_hi, o_lo = sem("o_ev"), sem("o_hi"), sem("o_lo")
        o_out = [sem(f"o_out{i}") for i in range(2)]
        first_in, first_hi, first_lo = (sem("first_" + n) for n in ("in", "hi", "lo"))
        p_in = [sem(f"p_in{i}") for i in range(len(OUT_CHUNKS))]
        p_hi, p_lo = sem("p_hi"), sem("p_lo")
        y_mm, x_add = sem("y_mm"), sem("x_add")
        h_mm, h_act, h_hi, h_lo = (sem("h_" + n) for n in ("mm", "act", "hi", "lo"))
        stored = sem("stored")
        act_waited, dve_waited, pool_waited, sp_waited = (sem(n + "_waited") for n in ("act", "dve", "pool", "sp"))

        block = ctx.enter_context(nc.Block())

        def schedule(eng, ln, contexts, query, attend, project, mlp):
            ln(0, 0)
            contexts(ATT0, 0)
            query(0, 0, 0, 0, A_Q0, 0)
            attend(ATT0, 0)
            project(0, 0, 0, 0, A_O0, 0, 0)
            ln(1, RT)
            mlp(0, 0, 1, RT)
            with eng.Fori(1, 3) as fg:
                mlp(0, fg, 1, RT * (fg + 1))
            mlp(0, 3, 1, RT * 4, True)
            with eng.Fori(0, 2) as a:
                ln(2 + a, 5 * RT + 4 * RT * a)
                contexts(ATT1, a)
                with eng.Fori(0, GROUPS // 2) as half:
                    for slot, first in ((0, A_L1), (1, B_L1)):
                        query(1, a, 2 * half + slot, slot, PER_LAYER * a + half + first, 1 + 4 * a + 2 * half + slot)
                attend(ATT1, a)
                for group in range(GROUPS):
                    slot = group % 2
                    project(1, a, group, slot, PER_LAYER * a + group // 2 + (B_L1 if slot else A_L1) + 6,
                            1 + 4 * a + group, 5 * RT + 4 * RT * a + RT * group)
            ln(4, 13 * RT)
            with eng.Fori(0, 2) as fg:
                mlp(1, fg, 4, 13 * RT + RT * fg)
            mlp(1, 2, 4, 15 * RT)
            mlp(1, 3, 4, 16 * RT)

        def batches(eng, att, a, prologue, one_batch):
            def pair(group, p, final=False):
                for parity in range(2):
                    one_batch(Place(att, a, group, p, parity, final))

            prologue(Place(att, a, 0, 0, 0))
            if att.layer == 0:
                pair(0, 0)
                with eng.Fori(1, PAIRS - 1) as p:
                    pair(0, p)
                pair(0, PAIRS - 1, final=True)
                return
            with eng.Fori(0, GROUPS - 1) as group:
                with eng.Fori(0, PAIRS - 1) as p:
                    pair(group, p)
                pair(group, PAIRS - 1)
            with eng.Fori(0, PAIRS - 1) as p:
                pair(GROUPS - 1, p)
            pair(GROUPS - 1, PAIRS - 1, final=True)

        def value_parts(place, t, j):
            return ([], []) if place.final else place.att.value_parts[place.swap].get((t, j), ([], []))

        def mlp_block(m, fg):
            return (A_M0, A_M1)[m] + fg, (B_M0, B_M1)[m] + fg

        def landing(c):
            return cs[c // 2][c % 2][:, 0:OUT_CHUNKS[c][1] * NT * LQ].bitcast(F32)

        def split_place(part, c):
            b0, nb = OUT_CHUNKS[c]
            return act_t[part][:, :, b0 * LQ:(b0 + nb) * LQ].rearrange("p t (b r) -> p b t r", b=nb)

        def skip(*_):
            return

        def exists(slot, n):
            return not isinstance(n, int) or n < (N_A, N_B)[slot]

        def cols(att):
            return col_b if att.layer else col_a

        @block.sync
        def _(sp):
            def load_block(slot, n, columns=range(NT)):
                if not exists(slot, n):
                    return
                src = (blocks_a, blocks_b)[slot][ds(n, 1)].rearrange("o p (k n) -> (o p) k n", k=DT)
                for t in columns:
                    wait(sp, w_lo[slot], 4 * (n - 1) + t + 1)
                    part = slice(t * P, (t + 1) * P)
                    sp.dma_start(w_raw[slot][:, :, part], src[:, :, part]).then_inc(w_in[slot], 16)

            def ln(e, x0):
                wait(sp, bias_add, RT * e)
                sp.dma_start(bias_row[:], row_bias[ds(e, 1), :].partition_broadcast(P)).then_inc(bias_in, 16)

            def query(layer, a, group, slot, n, step):
                for i in range(2 * NT):
                    t, half = i // 2, i % 2
                    sp.wait_ge(q_lo, 8 * step + i + 1)
                    for s in range(2):
                        src = q[half][s][:].bitcast(F32).rearrange("p (b r) -> p b r", b=NB // 2)
                        dst = q_scr[s][ds(group, 1), half * 4:half * 4 + 4, :, t * LQ:(t + 1) * LQ]
                        sp.dma_start(dst.rearrange("o b p r -> p (o b) r"), src).then_inc(q_out[half], 16)
                    if half:
                        load_block(slot, n + 2, [t])

            def load_q(place):
                wait(sp, s_mm, place.att.units_before(place.tile - NT))
                for s in range(2):
                    src = q_scr[s][ds(place.group, 1), ds(place.b, 1)].rearrange("g b p f -> (g b p) f")
                    sp.dma_start(q[place.parity][s][:].bitcast(F32), src).then_inc(q_in[place.parity], 16)

            def load_extra_value(place, buf):
                wait(sp, av_mm, place.att.units_before(place.tile - NT * (1 - buf)))
                src = xv_scr[ds(place.a, 1), ds(place.group, 1)].rearrange("a g f -> (a g) f")
                sp.dma_start(v[buf][LK - 256:LK - 255, 2, :], src).then_inc(xv_in[buf], 16)

            def attend(att, a):
                def prologue(place):
                    for half in range(2):
                        sp.wait_ge(q_out[half], 32 * NT * (1 + 4 * (a + 1) if att.layer else 1))
                    load_q(place)
                    if att.layer == 1:
                        for buf in range(2):
                            load_extra_value(place, buf)

                def one_batch(place):
                    after = None if place.final else place.next()
                    if after:
                        load_q(after)
                    if place.swap:
                        if after:
                            load_extra_value(after, 0)
                        load_block(0, place.block_a + 2)
                        load_block(1, place.block_b + 2)
                    if att.layer == 0:
                        return
                    if place.last_block:
                        for i in range(2):
                            sp.wait_ge(o_out[i], 16 * place.stores)
                        wait(sp, first_in, 16 * place.first)
                        dst = act_t[1][:, :, ds(place.b * LQ, LQ)].bitcast(F32)
                        src = o_scr[0, ds(place.b, 1)].rearrange("b p (t r) -> (b p) t r", t=NT)
                        sp.sem_inc(sp_waited, 1)
                        sp.dma_start(dst, src).then_inc(first_in, 16)
                    sp.wait_ge(o_ev, NT * place.batch + NT)
                    dst = o_scr[ds(place.group, 1), ds(place.b, 1)].rearrange("g b p f -> (g b p) f")
                    sp.dma_start(dst, o[place.parity][:, 0:NT * LQ]).then_inc(o_out[place.parity], 16)
                    if place.swap and after:
                        load_extra_value(after, 1)

                batches(sp, att, a, prologue, one_batch)

            def project(layer, a, group, slot, n, step, x0):
                for g in {0: (1, 2), 1: (3,)}.get(group, ()) if layer else ():
                    for i in range(2):
                        sp.wait_ge(o_out[i], 16 * PAIRS * GROUPS * (a + 1))
                    for c, (b0, nb) in enumerate(OUT_CHUNKS):
                        if g > 1:
                            sp.wait_ge(p_lo, 3 * (3 * a + g - 2) + c + 1)
                        src = o_scr[g, b0:b0 + nb].rearrange("b p f -> p b f")
                        sp.dma_start(landing(c).rearrange("p (b f) -> p b f", b=nb), src).then_inc(p_in[c], 16)
                load_block(slot, n + 2)

            def mlp(m, fg, e, x0, last=False):
                na, nb = mlp_block(m, fg)
                load_block(0, na + 2)
                load_block(1, nb + 2)
                if isinstance(fg, int) and m == 1 and fg == 3:
                    for r in range(RT):
                        sp.wait_ge(x_add, x0 + r + 1)
                        sp.dma_start(out[r * P:(r + 1) * P, :], x[:, r, :]).then_inc(stored, 16)
                    sp.wait_ge(stored, 16 * RT)

            sp.dma_start(x[:], x_in.rearrange("(r p) d -> p r d", p=P)).then_inc(start_in, 16)
            sp.dma_start(ident[:], eye).then_inc(vecs_in, 16)
            sp.dma_start(prob[0][0:N_CA, 0:P], vec_a).then_inc(vecs_in, 16)
            sp.dma_start(prob[0][:, P:2 * P], vec_b).then_inc(vecs_in, 16)
            sp.dma_start(prob[0][0:32, 2 * P:3 * P], value_rows).then_inc(vecs_in, 16)
            sp.dma_start(prob[0][0:32, 3 * P:4 * P], value_bias_rows).then_inc(vecs_in, 16)
            sp.dma_start(mask_u8[:], mask_in.partition_broadcast(LQ)).then_inc(vecs_in, 16)
            sp.wait_ge(start_in, 16)
            load_block(0, 0)
            sp.dma_start(ctx_t[:, :, 0:2 * KW], ctx_in[:, :, 0:2 * KW]).then_inc(ctx_in_sem[0], 16)
            load_block(1, 0)
            sp.wait_ge(xv_diff, 1)
            sp.dma_start(xv_scr.rearrange("a g (t n) -> (a g t) n", n=P), key_cap[0:32, 0:P]).then_inc(xv_out, 16)
            load_block(0, 1)
            sp.dma_start(ctx_t[:, :, 2 * KW:], ctx_in[:, :, 2 * KW:]).then_inc(ctx_in_sem[1], 16)
            load_block(1, 1)
            schedule(sp, ln, skip, query, attend, project, mlp)

        @block.gpsimd
        def _(pool):
            def split_lo(slot, n):
                if not exists(slot, n):
                    return
                for s in range(4):
                    pool.wait_ge(w_hi[slot], 4 * n + s + 1)
                    part = slice(s * P, (s + 1) * P)
                    pool.tensor_tensor(w[slot][1][:, :, part], w_raw[slot][:, :, part], w[slot][0][:, :, part],
                                       ALU.subtract).then_inc(w_lo[slot], 1)

            def ln(e, x0):
                pool.wait_ge(bias_in, 16 * e + 16)
                for r in range(RT):
                    pool.wait_ge(ln_xhat, RT * e + r + 1)
                    pool.tensor_tensor(x[:, r, :], x[:, r, :], bias_row[:], ALU.add).then_inc(bias_add, 1)

            def context_lo(place):
                pool.wait_ge(cs_hi, place.batch + 1)
                pool.tensor_tensor(cs[place.parity][1][:, 0:DT * KW].rearrange("p (k n) -> p k n", k=DT),
                                   ctx_t[:, :, ds(place.b * KW, KW)],
                                   cs[place.parity][0][:, 0:DT * KW].rearrange("p (k n) -> p k n", k=DT),
                                   ALU.subtract).then_inc(cs_lo, 1)

            def contexts(att, a):
                if att.layer == 0:
                    pool.wait_ge(ctx_in_sem[0], 16)
                else:
                    pool.wait_ge(y_mm, 5 * RT + 4 * RT * a)
                    pool.sem_inc(pool_waited, 1)
                for place in (Place(att, a, 0, 0, 0), Place(att, a, 0, 0, 1)):
                    pool.tensor_copy(cs[place.parity][0][:, 0:DT * KW].rearrange("p (k n) -> p k n", k=DT),
                                     ctx_t[:, :, ds(place.b * KW, KW)]).then_inc(cs_hi, 1)
                    context_lo(place)

            def attend(att, a):
                def extra_key(place, t):
                    col = 16 * place.a + NT * place.group + t
                    wait(pool, s_mm, att.units_before(place.tile + t - 1))
                    pool.sem_inc(pool_waited, 1)
                    pool.tensor_copy(k[t % 2][0][:, LK:KW], xk[0][:, ds(col, 1)])
                    pool.tensor_copy(k[t % 2][1][:, LK:KW], xk[1][:, ds(col, 1)]).then_inc(k_extra, 1)

                def output(place):
                    rows = ds(place.b * LQ, LQ)
                    z = o[place.parity][:, 0:NT * LQ].rearrange("p (t r) -> p t r", t=NT)
                    pool.wait_ge(o_ev, NT * place.batch + NT)
                    pool.sem_inc(pool_waited, 1)
                    pool.tensor_copy(act_t[0][:, :, rows], z).then_inc(o_hi, 1)
                    pool.wait_ge(o_hi, place.batch + 1)
                    pool.tensor_tensor(act_t[1][:, :, rows], z, act_t[0][:, :, rows], ALU.subtract).then_inc(o_lo, 1)

                def prologue(place):
                    if att.layer == 1:
                        for t in range(att.key_ahead):
                            extra_key(place, t)

                def one_batch(place):
                    for t in range(NT):
                        tile = place.key(t + att.key_ahead)
                        if att.layer == 1 and tile:
                            extra_key(*tile)
                        if t == att.context_slot[0] and place.after(2):
                            if att.layer == 0:
                                pool.wait_ge(ctx_in_sem[1], 16)
                            context_lo(place.after(2))
                    if att.layer == 0:
                        output(place)

                batches(pool, att, a, prologue, one_batch)

            def project(layer, a, group, slot, n, step, x0):
                split_lo(slot, n + 1)

            def mlp(m, fg, e, x0, last=False):
                na, nb = mlp_block(m, fg)
                split_lo(0, na + 1)
                split_lo(1, nb + 1)

            pool.wait_ge(w_in[0], 16 * NT)
            for s in range(4):
                part = slice(s * P, (s + 1) * P)
                pool.tensor_copy(w[0][0][:, :, part], w_raw[0][:, :, part]).then_inc(w_hi[0], 1)
            split_lo(0, 0)
            pool.wait_ge(vec_split, 2)
            schedule(pool, ln, contexts, skip, attend, project, mlp)

        @block.scalar
        def _(act):
            def split_hi(slot, n, subs, free):
                if not exists(slot, n):
                    return
                act.wait_ge(w_in[slot], 16 * NT * (n + 1))
                for s in subs:
                    if free:
                        act.wait_ge(*free(s))
                    act.activation(w[slot][0][:, :, s * P:(s + 1) * P], w_raw[slot][:, :, s * P:(s + 1) * P],
                                   ACT.Identity).then_inc(w_hi[slot], 1)

            def ln(e, x0):
                act.wait_ge(ln_eps, e + 1)
                act.activation(std[:], var_eps[:], ACT.Sqrt).then_inc(ln_std, 1)
                for r in range(RT):
                    act.wait_ge(ln_turn, RT * e + r + 1)
                    wait(act, ln_lo, RT * e + r - 1)
                    act.sem_inc(act_waited, 1)
                    for c in range(DT):
                        last = act.activation(o[r % 2][:, c * P:(c + 1) * P], ps_t[r % 2][:, c * P:(c + 1) * P], ACT.Identity,
                                              bias=col_a[:, ds(C_LN + 8 * e + 4 + c, 1)],
                                              scale=col_a[:, ds(C_LN + 8 * e + c, 1)])
                    last.then_inc(ln_act, 1)
                if isinstance(e, int) and e == 0:
                    split_hi(1, 0, range(4), None)

            def query(layer, a, group, slot, n, step):
                scale = float((HD1 if layer else HD0) ** -0.5)
                for i in range(2 * NT):
                    t, half = i // 2, i % 2
                    col = (N_CB1 * a + C_BQ1 if layer else C_BQ0) + NT * group + t
                    act.wait_ge(q_mm, 8 * step + i + 1)
                    wait(act, q_lo, 8 * step + i - 1)
                    act.sem_inc(act_waited, 1)
                    act.activation(prob[half][:, 0:HALF], ps_y[half][:, 0:HALF], ACT.Identity, scale=scale,
                                   bias=(col_b if layer else col_a)[:, ds(col, 1)]).then_inc(q_act, 1)
                    if half:
                        split_hi(slot, n + 1, [t], lambda s: (q_mm, 8 * step + 2 * s + 2))

            def attend(att, a):
                sub, layer = att.sub, att.layer

                def key_hi(place, t):
                    tile = place.tile + t
                    act.wait_ge(k_mm, tile + 1)
                    wait(act, s_mm, att.units_before(tile - 1))
                    act.sem_inc(act_waited, 1)
                    n = KW if layer == 0 else LK
                    act.activation(k[t % 2][0][:, 0:n], ps_k[:, 0:n], ACT.Identity,
                                   bias=cols(att)[:, ds(place.column((C_BK0, C_BK1), t), 1)]).then_inc(k_hi, 1)

                def value(place, i):
                    n = KEY_TILES[i][1]
                    act.wait_ge(v_mm, 3 * place.batch + i + 1)
                    wait(act, av_mm, att.units_before(place.tile - NT))
                    act.activation(v[place.parity][0:n, i, :], ps_v[0:n, :], ACT.Identity).then_inc(v_ev, 1)

                def value_ends(place, parts):
                    for i, _, end in parts:
                        if end == DT:
                            value(place.next(), i)

                def turned(place, t, j):
                    unit, buf = place.unit + sub * t + j, (j if layer == 0 else t) % 2
                    act.wait_ge(t_mm, unit + 1)
                    wait(act, av_mm, unit - 1)
                    act.activation(prob_t[buf][:], ps_t[buf][:, 0:3 * LQ], ACT.Identity).then_inc(t_ev, 1)

                def exp(place, t, j):
                    unit, buf = place.unit + sub * t + j, (j if layer == 0 else t) % 2
                    act.wait_ge(s_max, unit + 1)
                    wait(act, t_mm, unit - 1)
                    src = ps_s[buf] if layer else prob[buf]
                    act.activation(prob[buf][0:LQ, 0:att.keys], src[0:LQ, 0:att.keys], ACT.Exp,
                                   bias=max_neg[0:LQ, buf:buf + 1],
                                   accum_out=prob_sum[0:LQ, buf:buf + 1]).then_inc(s_exp, 1)

                def output(place, t):
                    act.wait_ge(av_mm, att.units_before(place.tile + t + 1))
                    if t == 0:
                        if layer == 0:
                            wait(act, o_lo, place.batch - 1)
                        else:
                            wait(act, o_out[place.parity], 16 * place.stores)
                    act.sem_inc(act_waited, 1)
                    act.activation(o[place.parity][:, t * LQ:(t + 1) * LQ], ps_o[t % 2][:, 0:LQ],
                                   ACT.Identity, bias=cols(att)[:, ds(place.column((C_BV0, C_BV1), t), 1)])\
                        .then_inc(o_ev, 1)

                def first_outputs(place):
                    rows = ds(place.b * LQ, LQ)
                    act.wait_ge(first_in, 16 * place.first + 16)
                    act.sem_inc(act_waited, 1)
                    act.activation(act_t[0][:, :, rows], act_t[1][:, :, rows].bitcast(F32), ACT.Identity)\
                        .then_inc(first_hi, 1)

                def prologue(place):
                    if layer == 0:
                        for i in range(3):
                            value(place, i)
                    key_hi(place, 0)
                    key_hi(place, 1)
                    if layer == 1:
                        for i in range(3):
                            value(place, i)
                    exp(place, 0, 0)
                    if layer == 1:
                        key_hi(place, 2)
                    exp(*place.at(0, 0, 1))
                    turned(place, 0, 0)

                def one_batch(place):
                    for t in range(NT):
                        for j in range(sub):
                            value_ends(place, value_parts(place, t, j)[0])
                            if j == att.key_slot and place.key(t + att.key_ahead):
                                key_hi(*place.key(t + att.key_ahead))
                            if place.at(t, j, 1):
                                turned(*place.at(t, j, 1))
                            if place.at(t, j, 2):
                                exp(*place.at(t, j, 2))
                            if j == sub - 1 and place.split_column(t) is not None:
                                split_hi(0, place.block_a + 1, [place.split_column(t)],
                                         lambda s: (k_mm, place.tile + NT * (1 - place.parity) + s + 1))
                            if j == sub - 1:
                                output(place, t)
                            value_ends(place, value_parts(place, t, j)[1])
                            if place.swap and (t, j) == (0, 0):
                                split_hi(1, place.block_b + 1, range(4), lambda s: (v_mm, 3 * place.batch + 3))
                            if place.last_block and t == 2:
                                first_outputs(place)

                batches(act, att, a, prologue, one_batch)

            def project(layer, a, group, slot, n, step, x0):
                if layer and group + 1 < GROUPS:
                    for c in range(len(OUT_CHUNKS)):
                        act.wait_ge(p_in[c], 16 * (3 * a + group + 1))
                        act.wait_ge(y_mm, x0 + CHUNK_FREE[c])
                        act.activation(split_place(0, c), landing(c).rearrange("p (b t r) -> p b t r", t=NT, r=LQ),
                                       ACT.Identity).then_inc(p_hi, 1)
                split_hi(slot, n + 1, range(4), lambda s: (y_mm, x0 + RT))

            def mlp(m, fg, e, x0, last=False):
                na, nb = mlp_block(m, fg)
                for c, (r0, nr) in enumerate(MLP_CHUNKS):
                    for f in range(4):
                        u = 12 * (4 * m + fg) + 4 * c + f
                        col = (C_FC0, C_FC1)[m] + 4 * fg + f
                        act.wait_ge(h_mm, u + 1)
                        wait(act, h_lo, u - 1)
                        act.sem_inc(act_waited, 1)
                        act.activation(prob[f % 2][:, 0:nr], ps_s[f % 2][:, 0:nr],
                                       ACT.Gelu if m else ACT.Gelu_apprx_tanh,
                                       bias=col_a[:, ds(col, 1)]).then_inc(h_act, 1)
                split_hi(0, na + 1, range(4), lambda s: (h_mm, 12 * (4 * m + fg) + 8 + s + 1))
                split_hi(1, nb + 1, range(4), lambda s: (y_mm, x0 + RT))

            act.wait_ge(vec_ev, 4)
            schedule(act, ln, skip, query, attend, project, mlp)

        @block.vector
        def _(dve):
            def split_lo(slot, n, subs):
                if not exists(slot, n):
                    return
                for s in subs:
                    dve.wait_ge(w_hi[slot], 4 * n + s + 1)
                    part = slice(s * P, (s + 1) * P)
                    dve.tensor_tensor(w[slot][1][:, :, part], w_raw[slot][:, :, part], w[slot][0][:, :, part],
                                      ALU.subtract).then_inc(w_lo[slot], 1)

            def statistics(r, e):
                dve.bn_stats(stats[:, r, :], x[:, r, :]).then_inc(ln_stat, 1)
                if r:
                    mean_variance(r - 1, e)

            def mean_variance(r, e):
                dve.wait_ge(ln_stat, RT * e + r + 1)
                dve.sem_inc(dve_waited, 1)
                dve.bn_aggr(mean_var[:, r, :], stats[:, r, :]).then_inc(ln_agg, 1)

            def ln(e, x0):
                if isinstance(e, int) and e == 0:
                    dve.wait_ge(start_in, 16)
                    for r in range(RT):
                        statistics(r, e)
                mean_variance(RT - 1, e)
                dve.wait_ge(ln_agg, RT * e + RT)
                dve.tensor_scalar(var_eps[:], mean_var[:, :, 1], EPS, None, ALU.add).then_inc(ln_eps, 1)
                dve.wait_ge(ln_std, e + 1)
                dve.reciprocal(rstd[:], std[:]).then_inc(ln_rstd, 1)
                dve.wait_ge(ln_rstd, e + 1)

                def normalized(r):
                    wait(dve, ln_turn, RT * e + r - 1)
                    dve.tensor_scalar(prob[r % 2][:], x[:, r, :], mean_var[:, r, 0:1], rstd[:, r:r + 1],
                                      ALU.subtract, ALU.mult).then_inc(ln_xhat, 1)

                normalized(0)
                normalized(1)
                for r in range(RT):
                    z = o[r % 2][:].rearrange("p (k n) -> p k n", k=DT)
                    dve.wait_ge(ln_act, RT * e + r + 1)
                    dve.tensor_copy(act_t[0][:, :, r * P:(r + 1) * P], z).then_inc(ln_hi, 1)
                    if r + 2 < RT:
                        normalized(r + 2)
                    dve.wait_ge(ln_hi, RT * e + r + 1)
                    dve.tensor_tensor(act_t[1][:, :, r * P:(r + 1) * P], z, act_t[0][:, :, r * P:(r + 1) * P],
                                      ALU.subtract).then_inc(ln_lo, 1)
                if isinstance(e, int) and e == 0:
                    split_lo(1, 0, range(4))

            def query(layer, a, group, slot, n, step):
                for i in range(2 * NT):
                    t, half = i // 2, i % 2
                    hi, lo = (q[half][s][:] for s in range(2))
                    dve.wait_ge(q_act, 8 * step + i + 1)
                    wait(dve, q_out[half], 32 * (4 * step + t))
                    dve.tensor_copy(hi, prob[half][:, 0:HALF]).then_inc(q_hi, 1)
                    dve.wait_ge(q_hi, 8 * step + i + 1)
                    dve.tensor_tensor(lo, prob[half][:, 0:HALF], hi, ALU.subtract).then_inc(q_lo, 1)
                    if half:
                        split_lo(slot, n + 1, [t])

            def attend(att, a):
                sub, layer = att.sub, att.layer

                def context_hi(place):
                    if layer == 0:
                        dve.wait_ge(ctx_in_sem[1], 16)
                    wait(dve, k_mm, place.tile - NT)
                    dve.tensor_copy(cs[place.parity][0][:, 0:DT * KW].rearrange("p (k n) -> p k n", k=DT),
                                    ctx_t[:, :, ds(place.b * KW, KW)]).then_inc(cs_hi, 1)

                def key_lo(place, t):
                    n = KW if layer == 0 else LK
                    dve.wait_ge(k_hi, place.tile + t + 1)
                    dve.scalar_tensor_tensor(out=k[t % 2][1][:, 0:n], in0=ps_k[:, 0:n],
                                             scalar=cols(att)[:, ds(place.column((C_BK0, C_BK1), t), 1)],
                                             in1=k[t % 2][0][:, 0:n], op0=ALU.add, op1=ALU.subtract).then_inc(k_lo, 1)

                def key_caps(place):
                    dve.tensor_scalar(key_cap[:], mask_u8[:, ds(place.b * LK, LK)], -0.5, LARGEST,
                                      ALU.add, ALU.mult).then_inc(cap_half, 1)
                    dve.wait_ge(cap_half, place.batch + 1)
                    dve.tensor_scalar(key_cap[:], key_cap[:], 2.0, None, ALU.mult).then_inc(cap_full, 1)
                    dve.wait_ge(cap_full, place.batch + 1)

                def maximum(place, t, j):
                    unit, buf = place.unit + sub * t + j, (j if layer == 0 else t) % 2
                    dve.wait_ge(s_mm, unit + 1)
                    neg = max_neg[0:LQ, buf:buf + 1]
                    if layer:
                        dve.tensor_reduce(neg, ps_s[buf][0:LQ, 0:KW], AX_X, ALU.max, negate=True).then_inc(s_max, 1)
                        return
                    if (t, j) == (0, 0):
                        key_caps(place)
                    masked = prob[buf][0:LQ, 0:LK]
                    wait(dve, t_mm, unit - 1)
                    dve.tensor_tensor(masked, ps_s[buf][0:LQ, 0:LK], key_cap[:], ALU.min).then_inc(s_cap, 1)
                    dve.wait_ge(s_cap, unit + 1)
                    dve.tensor_reduce(neg, masked, AX_X, ALU.max, negate=True).then_inc(s_max, 1)

                def normalize(place, t, j):
                    unit, buf = place.unit + sub * t + j, (j if layer == 0 else t) % 2
                    dve.wait_ge(s_exp, unit + 1)
                    dve.reciprocal(prob_rcp[0:LQ, buf:buf + 1], prob_sum[0:LQ, buf:buf + 1]).then_inc(s_rcp, 1)
                    dve.wait_ge(s_rcp, unit + 1)
                    dve.tensor_scalar(prob[buf][0:LQ, 0:att.keys], prob[buf][0:LQ, 0:att.keys],
                                      prob_rcp[0:LQ, buf:buf + 1], None, ALU.mult).then_inc(s_norm, 1)

                def first_outputs(place):
                    rows = ds(place.b * LQ, LQ)
                    dve.wait_ge(first_hi, place.first + 1)
                    dve.tensor_tensor(act_t[1][:, :, rows], act_t[1][:, :, rows].bitcast(F32), act_t[0][:, :, rows],
                                      ALU.subtract).then_inc(first_lo, 1)

                def prologue(place):
                    key_lo(place, 0)
                    key_lo(place, 1)
                    maximum(place, 0, 0)
                    if layer == 0:
                        maximum(place, 0, 1)
                    normalize(place, 0, 0)
                    if layer == 1:
                        key_lo(place, 2)
                        maximum(place, 1, 0)
                    normalize(*place.at(0, 0, 1))
                    if layer == 0:
                        maximum(place, 0, 2)

                def one_batch(place):
                    for t in range(NT):
                        for j in range(sub):
                            if j == att.key_slot and place.key(t + att.key_ahead):
                                key_lo(*place.key(t + att.key_ahead))
                            if layer == 1 and place.at(t, j, 2):
                                maximum(*place.at(t, j, 2))
                            if place.at(t, j, 2):
                                normalize(*place.at(t, j, 2))
                            if layer == 0 and place.at(t, j, 3):
                                maximum(*place.at(t, j, 3))
                            if j == sub - 1 and place.split_column(t) is not None:
                                split_lo(0, place.block_a + 1, [place.split_column(t)])
                            if (t, j) == att.context_slot and place.after(2):
                                context_hi(place.after(2))
                            if place.swap and (t, j) == (0, 0):
                                split_lo(1, place.block_b + 1, range(4))
                            if place.last_block and t == 2:
                                first_outputs(place)

                batches(dve, att, a, prologue, one_batch)

            def add_y(r, e, x0, last):
                dve.wait_ge(y_mm, x0 + r + 1)
                dve.wait_ge(bias_add, RT * e + r + 1)
                wait(dve, x_add, x0 + r + 1 - RT)
                dve.tensor_tensor(x[:, r, :], ps_y[r % 2][:], x[:, r, :], ALU.add).then_inc(x_add, 1)
                if last:
                    dve.wait_ge(x_add, x0 + r + 1)
                    statistics(r, e + 1)

            def project(layer, a, group, slot, n, step, x0):
                more = layer and group + 1 < GROUPS
                for r in range(RT):
                    add_y(r, 2 + a if layer else 0, x0, not more)
                    if more and r + 1 in CHUNK_FREE:
                        c = CHUNK_FREE.index(r + 1)
                        dve.wait_ge(p_hi, 3 * (3 * a + group) + c + 1)
                        dve.tensor_tensor(split_place(1, c), landing(c).rearrange("p (b t r) -> p b t r", t=NT, r=LQ),
                                          split_place(0, c), ALU.subtract).then_inc(p_lo, 1)

            def mlp(m, fg, e, x0, last=False):
                na, nb = mlp_block(m, fg)

                def hidden(c):
                    r0, nr = MLP_CHUNKS[c]
                    wait(dve, y_mm, x0 + MLP_CHUNKS[0][1] // P if c == 2 else x0)
                    for f in range(4):
                        u = 12 * (4 * m + fg) + 4 * c + f
                        hi, lo = (cs[c % 2][s][:, f * CHUNK_MAX:f * CHUNK_MAX + nr] for s in range(2))
                        dve.wait_ge(h_act, u + 1)
                        dve.tensor_copy(hi, prob[f % 2][:, 0:nr]).then_inc(h_hi, 1)
                        dve.wait_ge(h_hi, u + 1)
                        dve.tensor_tensor(lo, prob[f % 2][:, 0:nr], hi, ALU.subtract).then_inc(h_lo, 1)

                def add_chunk(c):
                    r0, nr = MLP_CHUNKS[c]
                    for r in range(r0 // P, (r0 + nr) // P):
                        add_y(r, e, x0, last)

                hidden(0)
                hidden(1)
                add_chunk(0)
                hidden(2)
                add_chunk(1)
                add_chunk(2)

            for i in range(2):
                last = dve.memset(ps_t[i][:], 0.0)
            last.then_inc(cleared, 1)
            dve.wait_ge(vec_t, 1)
            dve.wait_ge(cleared, 1)
            dve.tensor_scalar(col_a[:, 0:NT], ps_t[0][:, 0:NT], float(HD0 ** -0.5), None, ALU.mult).then_inc(vec_ev, 1)
            dve.tensor_copy(col_a[:, NT:N_CA], ps_t[0][:, NT:N_CA]).then_inc(vec_ev, 1)
            by_layer = [t.rearrange("p (a c) -> p a c", a=2) for t in (col_b[:], ps_t[1][:, 0:P])]
            dve.tensor_scalar(by_layer[0][:, :, 0:16], by_layer[1][:, :, 0:16], float(HD1 ** -0.5), None,
                              ALU.mult).then_inc(vec_ev, 1)
            dve.tensor_copy(by_layer[0][:, :, 16:N_CB1], by_layer[1][:, :, 16:N_CB1]).then_inc(vec_ev, 1)
            dve.wait_ge(vec_ev, 4)
            extra = [t.rearrange("p (a c) -> p a c", a=2) for t in (xk[0][:], xk[1][:])]
            dve.tensor_copy(extra[0], by_layer[0][:, :, C_XK1:N_CB1]).then_inc(vec_split, 1)
            dve.wait_ge(vec_split, 1)
            dve.tensor_tensor(extra[1], by_layer[0][:, :, C_XK1:N_CB1], extra[0], ALU.subtract).then_inc(vec_split, 1)
            dve.tensor_tensor(key_cap[0:32, 0:P], prob[0][0:32, 2 * P:3 * P], prob[0][0:32, 3 * P:4 * P],
                              ALU.subtract).then_inc(xv_diff, 1)
            dve.wait_ge(xv_out, 16)
            dve.wait_ge(xv_diff, 1)
            schedule(dve, ln, skip, query, attend, project, mlp)

        @block.tensor
        def _(pe):
            def product(out, stationary, moving, first, last):
                (w_h, w_l), (m_h, m_l) = stationary, moving
                pe.matmul(out, w_h, m_h, start=first, stop=False)
                pe.matmul(out, w_h, m_l, start=False, stop=False)
                return pe.matmul(out, w_l, m_h, start=False, stop=last)

            def ln(e, x0):
                for r in range(RT):
                    pe.wait_ge(ln_xhat, RT * e + r + 1)
                    wait(pe, ln_act, RT * e + r - 1)
                    if isinstance(e, int) and e == 0:
                        pe.wait_ge(vec_ev, 4)
                    for c in range(DT):
                        last = pe.transpose(ps_t[r % 2][:, c * P:(c + 1) * P], prob[r % 2][:, c * P:(c + 1) * P], ident[:])
                    last.then_inc(ln_turn, 1)

            def query(layer, a, group, slot, n, step):
                for i in range(2 * NT):
                    t, half = i // 2, i % 2
                    if t == 0:
                        pe.wait_ge(ln_lo, RT * (2 + a if layer else 0) + (RT if half else -(-HALF // P)))
                    pe.wait_ge(w_lo[slot], 4 * n + t + 1)
                    wait(pe, q_act, 8 * step + i - 1)
                    for c in range(DT):
                        last = product(ps_y[half][:, 0:HALF],
                                       [w[slot][s][:, c, t * P:(t + 1) * P] for s in range(2)],
                                       [act_t[s][:, c, half * HALF:(half + 1) * HALF] for s in range(2)],
                                       c == 0, c == DT - 1)
                    last.then_inc(q_mm, 1)

            def attend(att, a):
                sub, layer = att.sub, att.layer

                def context_ready(place):
                    pe.wait_ge(cs_hi, place.batch + 1)
                    pe.wait_ge(cs_lo, place.batch + 1)

                def key(place, t, part=(0, DT)):
                    tile = place.tile + t
                    if part[0] == 0:
                        if t == 0:
                            context_ready(place)
                        pe.wait_ge(w_lo[0], 4 * place.block_a + t + 1)
                        wait(pe, k_lo, tile)
                    for c in range(*part):
                        last = product(ps_k[:, 0:KW],
                                       [w[0][s][:, c, t * P:(t + 1) * P] for s in range(2)],
                                       [cs[place.parity][s][:, c * KW:(c + 1) * KW] for s in range(2)],
                                       c == 0, c == DT - 1)
                    if part[1] == DT:
                        last.then_inc(k_mm, 1)

                def value(place, i, start=0, end=DT):
                    if start == 0:
                        if i == 0:
                            context_ready(place)
                            pe.wait_ge(w_lo[1], 4 * place.block_b + 4)
                        wait(pe, v_ev, 3 * place.batch + i)
                    k0, n = KEY_TILES[i]
                    for c in range(start, end):
                        last = product(ps_v[0:n, :],
                                       [cs[place.parity][s][:, c * KW + k0:c * KW + k0 + n] for s in range(2)],
                                       [w[1][s][:, c, :] for s in range(2)], c == 0, c == DT - 1)
                    if end == DT:
                        last.then_inc(v_mm, 1)

                def scores(place, t, j):
                    unit, buf = place.unit + sub * t + j, (j if layer == 0 else t) % 2
                    if j == 0:
                        pe.wait_ge(k_lo, place.tile + t + 1)
                        if layer:
                            pe.wait_ge(k_extra, place.tile + t + 1 - att.tile0)
                    if (t, j) == (0, 0):
                        pe.wait_ge(q_in[place.parity], 32 * place.same_parity + 32)
                    wait(pe, s_exp if layer else s_cap, unit - 1)
                    rows = slice(0, P) if layer else slice(HD0 * j, HD0 * (j + 1))
                    product(ps_s[buf][0:LQ, 0:KW],
                            [q[place.parity][s][rows, t * LQ:(t + 1) * LQ] for s in range(2)],
                            [k[t % 2][s][rows, :] for s in range(2)], True, True).then_inc(s_mm, 1)

                def turn(place, t, j):
                    unit, buf = place.unit + sub * t + j, (j if layer == 0 else t) % 2
                    pe.wait_ge(s_norm, unit + 1)
                    wait(pe, t_ev, unit - 1)
                    for i, n in enumerate(att.vals()):
                        last = pe.transpose(ps_t[buf][0:n, i * LQ:(i + 1) * LQ],
                                            prob[buf][0:LQ, i * P:i * P + n], ident[0:LQ, 0:LQ])
                    last.then_inc(t_mm, 1)

                def weighted(place, t, j):
                    unit, buf = place.unit + sub * t + j, (j if layer == 0 else t) % 2
                    if (t, j) == (0, 0):
                        pe.wait_ge(v_ev, 3 * place.batch + 3)
                        if layer:
                            pe.wait_ge(xv_in[place.parity], 16 * place.block + 16)
                    if j == 0:
                        wait(pe, o_ev, NT * place.batch + t - 1)
                    pe.wait_ge(t_ev, unit + 1)
                    rows = slice(0, P) if layer else slice(HD0 * j, HD0 * (j + 1))
                    for i, n in enumerate(att.vals()):
                        last = pe.matmul(ps_o[t % 2][rows, 0:LQ],
                                         v[place.parity][0:n, i, t * P + rows.start:t * P + rows.stop],
                                         prob_t[buf][0:n, i * LQ:(i + 1) * LQ], start=(i == 0), stop=(i == 2))
                    last.then_inc(av_mm, 1)

                def prologue(place):
                    pe.wait_ge(q_act, 8 * (1 + 4 * (a + 1) if layer else 1))
                    if layer == 0:
                        for i in range(3):
                            value(place, i)
                    key(place, 0)
                    key(place, 1)
                    if layer == 1:
                        for i in range(3):
                            value(place, i)
                    scores(place, 0, 0)
                    if layer == 1:
                        key(place, 2)
                    for unit in range(1, att.score_ahead):
                        scores(*place.at(0, 0, unit))
                    turn(place, 0, 0)

                def one_batch(place):
                    for t in range(NT):
                        for j in range(sub):
                            for part in value_parts(place, t, j)[0]:
                                value(place.next(), *part)
                            if j in att.key_parts and place.key(t + att.key_ahead):
                                key(*place.key(t + att.key_ahead), att.key_parts[j])
                            if place.at(t, j, 1):
                                turn(*place.at(t, j, 1))
                            if place.at(t, j, att.score_ahead):
                                scores(*place.at(t, j, att.score_ahead))
                            weighted(place, t, j)
                            for part in value_parts(place, t, j)[1]:
                                value(place.next(), *part)

                batches(pe, att, a, prologue, one_batch)

            def bank_read(r, x0):
                wait(pe, x_add, x0 + r - 1 if r else x0)

            def project(layer, a, group, slot, n, step, x0):
                pe.wait_ge(w_lo[slot], 4 * n + 4)
                for r in range(RT):
                    if group == 0:
                        pe.wait_ge(first_lo if layer else o_lo, NB * a + -(-(r + 1) * P // LQ))
                    if layer and group:
                        pe.wait_ge(p_lo, 3 * (3 * a + group - 1) + CHUNK_OF[r] + 1)
                    bank_read(r, x0)
                    for t in range(NT):
                        last = product(ps_y[r % 2][:], [act_t[s][:, t, r * P:(r + 1) * P] for s in range(2)],
                                       [w[slot][s][:, t, :] for s in range(2)], t == 0, t == NT - 1)
                    last.then_inc(y_mm, 1)

            def mlp(m, fg, e, x0, last=False):
                na, nb = mlp_block(m, fg)

                def up(c):
                    r0, nr = MLP_CHUNKS[c]
                    pe.wait_ge(ln_lo, RT * e + (r0 + nr) // P)
                    for f in range(4):
                        u = 12 * (4 * m + fg) + 4 * c + f
                        pe.wait_ge(w_lo[0], 4 * na + f + 1)
                        wait(pe, h_act, u - 1)
                        for t in range(DT):
                            last = product(ps_s[f % 2][:, 0:nr], [w[0][s][:, t, f * P:(f + 1) * P] for s in range(2)],
                                           [act_t[s][:, t, r0:r0 + nr] for s in range(2)], t == 0, t == DT - 1)
                        last.then_inc(h_mm, 1)

                def down(c):
                    r0, nr = MLP_CHUNKS[c]
                    pe.wait_ge(h_lo, 12 * (4 * m + fg) + 4 * c + 4)
                    pe.wait_ge(w_lo[1], 4 * nb + 4)
                    for i in range(nr // P):
                        r = r0 // P + i
                        bank_read(r, x0)
                        for f in range(4):
                            at = f * CHUNK_MAX + i * P
                            last = product(ps_y[r % 2][:], [cs[c % 2][s][:, at:at + P] for s in range(2)],
                                           [w[1][s][:, f, :] for s in range(2)], f == 0, f == 3)
                        last.then_inc(y_mm, 1)

                up(0)
                up(1)
                down(0)
                up(2)
                down(1)
                down(2)

            pe.wait_ge(vecs_in, 16 * 6)
            pe.wait_ge(cleared, 1)
            pe.transpose(ps_t[0][:, 0:N_CA], prob[0][0:N_CA, 0:P], ident[0:N_CA, 0:N_CA])
            pe.transpose(ps_t[1][:, 0:P], prob[0][:, P:2 * P], ident[:]).then_inc(vec_t, 1)
            schedule(pe, ln, skip, query, attend, project, mlp)


def kernel(**inputs):
    import numpy as np
    import concourse.bacc as bacc
    from concourse.bass_utils import run_bass_kernel_spmd

    g = {name: np.asarray(value) for name, value in inputs.items()}
    l0, l1 = (lambda n: g["L0_xattn_" + n]), (lambda n: g["L1_xattn_" + n])

    def blocks(weight):
        rows, columns = weight.shape
        if rows == D:
            b = weight.reshape(DT, P, columns // D, D).transpose(2, 1, 0, 3)
        else:
            b = weight.reshape(rows // D, DT, P, D).transpose(0, 2, 1, 3)
        return list(b.reshape(-1, P, DT * D))

    a = blocks(l0("q_w")) + blocks(l0("k_w")) + blocks(l0("cproj_w")) + blocks(l0("fc_w"))
    b = blocks(l0("v_w")) + blocks(l0("proj_w"))
    for i in "12":
        wq, wk, wv, wo = (blocks(l1(f"w{m}{i}")) for m in "qkvo")
        a += wq[0::2] + wk + wo[0::2]
        b += wq[1::2] + wv + wo[1::2]
    a += blocks(l1("w_fc1"))
    b += blocks(l1("w_fc2"))
    blocks_a, blocks_b = np.stack(a), np.stack(b)

    def rows(*names):
        return np.concatenate([g[n].reshape(-1, P) for n in names])

    vec_a = rows("L0_xattn_q_b", "L0_xattn_k_b", "L0_xattn_v_b", "L0_xattn_fc_b", "L1_xattn_b_fc1",
                 "L0_xattn_ln1_w", "L0_xattn_ln1_b", "L0_xattn_ln2_w", "L0_xattn_ln2_b",
                 "L1_xattn_ln1_scale", "L1_xattn_ln1_offset", "L1_xattn_ln2_scale", "L1_xattn_ln2_offset",
                 "L1_xattn_ln_mlp_scale", "L1_xattn_ln_mlp_offset")
    vec_b = rows(*(f"L1_xattn_{n}{i}" for i in "12" for n in ("bq", "bk", "bv", "bias_k")))
    ctx = np.zeros((P, DT, NB, KW), g["ctx_2048"].dtype)
    ctx[:, :, :, 0:LK] = g["ctx_2048"].transpose(2, 0, 1).reshape(DT, P, NB, LK).transpose(1, 0, 2, 3)
    arrays = {
        "x": g["x"].reshape(ROWS, D),
        "ctx_t": ctx.reshape(P, DT, NB * KW),
        "mask": g["mask_BxS2_bf1"].reshape(1, NB * LK).view(np.uint8),
        "blocks_a": blocks_a, "blocks_b": blocks_b, "vec_a": vec_a, "vec_b": vec_b,
        "value_rows": rows("L1_xattn_bias_v1", "L1_xattn_bias_v2"),
        "value_bias_rows": rows("L1_xattn_bv1", "L1_xattn_bv2"),
        "row_bias": np.stack([l0("cproj_b"), l0("proj_b"), l1("bo1"), l1("bo2"), l1("b_fc2")]),
        "eye": np.eye(P, dtype=np.float32),
    }
    nc = bacc.Bacc("TRN2", target_bir_lowering=False, num_devices=1)
    arrays = {f"in_{n}": np.ascontiguousarray(v) for n, v in arrays.items()}
    args = [nc.dram_tensor(n, v.shape, mybir.dt.from_np(v.dtype), kind="ExternalInput").ap() for n, v in arrays.items()]
    out = nc.dram_tensor("out", (ROWS, D), F32, kind="ExternalOutput").ap()
    build(nc, *args, out)
    result = run_bass_kernel_spmd(nc, [arrays], core_ids=[0])
    return result.results[0]["out"].reshape(NB, LQ, D)
```

```python
from contextlib import ExitStack

import concourse.bass as bass
from concourse import mybir

F32 = mybir.dt.float32
F32R = mybir.dt.float32r
U8 = mybir.dt.uint8
ACT = mybir.ActivationFunctionType
ALU = mybir.AluOpType
AX_X = mybir.AxisListType.X
ds = bass.ds

P = 128
NB = 8
LQ = 112
LK = 375
KW = LK + 1
D = 512
DT = D // P
ROWS = NB * LQ
RT = ROWS // P
HALF = ROWS // 2
KEY_TILES = [(0, 128), (128, 128), (256, LK - 256)]
GROUPS = 4
PAIRS = NB // 2
NT = 4
SUB0 = 4
HD0, HD1 = 32, 128
EPS = 1e-5
LARGEST = 3.4028234663852886e38

A_Q0, A_K0, A_M0 = 0, 1, 2
B_V0, B_O0, B_M0 = 0, 1, 2
A_L1, B_L1, PER_LAYER = A_M0 + 4, B_M0 + 4, 8
A_M1, B_M1 = A_L1 + 2 * PER_LAYER, B_L1 + 2 * PER_LAYER
N_A, N_B = A_M1 + 4, B_M1 + 4

C_BQ0, C_BK0, C_BV0, C_FC0, C_FC1, C_LN = 0, 4, 8, 12, 28, 44
N_CA = C_LN + 8 * 5
C_BQ1, C_BK1, C_BV1, C_XK1, N_CB1 = 0, 16, 32, 48, 64

OUT_CHUNKS = [(0, 3), (3, 3), (6, 2)]
CHUNK_FREE = [-(-(b0 + nb) * LQ // P) for b0, nb in OUT_CHUNKS]
CHUNK_OF = [min(c for c, (b0, nb) in enumerate(OUT_CHUNKS) if (r + 1) * P <= (b0 + nb) * LQ) for r in range(RT)]
MLP_CHUNKS = [(0, 384), (384, 256), (640, 256)]
CHUNK_MAX = 384
X_PARTS = [(0, 4), (4, RT)]


class Attention:

    def __init__(self, layer, sub, tile0, unit0, batch0):
        self.layer, self.sub = layer, sub
        self.tile0, self.unit0, self.batch0 = tile0, unit0, batch0
        self.score_ahead, self.exp_ahead = (4, 3) if layer == 0 else (2, 2)
        self.key_ahead = 2 if layer == 0 else 3
        self.key_parts = {0: (0, 2), 1: (2, DT)} if layer == 0 else {0: (0, DT)}
        self.key_slot = max(self.key_parts)
        self.split_slots_b = {(NB - 1, 0): range(4)} if layer == 0 else {(NB - 2, 3): (0, 1), (NB - 1, 0): (2, 3)}
        self.split_slots = {(NB - 1, t): t for t in range(NT)} if layer == 0 else {
            (NB - 2, 2): 0, (NB - 2, 3): 1, (NB - 1, 0): 2, (NB - 1, 1): 3}
        if layer == 0:
            even = {(0, 2): ([], [(0, 0, 1)]), (0, 3): ([(0, 1, 2)], [(0, 2, 3)]),
                    (1, 2): ([(0, 3, DT)], []), (1, 3): ([(1, 0, 1)], [(1, 1, 2)]),
                    (2, 2): ([(1, 2, 3)], [(1, 3, DT)]), (2, 3): ([], [(2, 0, 1)]),
                    (3, 2): ([(2, 1, 2)], [(2, 2, 3)]), (3, 3): ([(2, 3, DT)], [])}
            late = {}
        else:
            even = {(0, 0): ([], [(0, 0, 3)]), (1, 0): ([(0, 3, DT)], [(1, 0, 2)]),
                    (2, 0): ([(1, 2, DT)], [(2, 0, 1)]), (3, 0): ([(2, 1, 3)], [(2, 3, DT)])}
            late = {(t, 0): ([], [(t - 1, 0, DT)]) for t in range(1, NT)}
        self.value_parts = {True: late, False: even}
        self.context_slot = (2, 0) if layer == 0 else (1, 0)
        self.query_slot = (1, 2) if layer == 0 else (1, 0)
        self.keys = LK if layer == 0 else KW

    def units_before(self, tile):
        return self.unit0 + self.sub * (tile - self.tile0)

    def vals(self):
        return [n if i < 2 else n + self.layer for i, (_, n) in enumerate(KEY_TILES)]


class Place:

    def __init__(self, att, a, group, pair, parity, final=False):
        self.att, self.a, self.group, self.pair, self.parity = att, a, group, pair, parity
        self.b = 2 * pair + parity
        self.swap = isinstance(self.b, int) and self.b == NB - 1
        self.last_block = att.layer == 1 and isinstance(group, int) and group == GROUPS - 1
        self.first = NB * a + self.b
        self.final_pair = final
        self.final = final and self.swap
        blocks = a * GROUPS + group
        self.batch = att.batch0 + blocks * NB + self.b
        self.same_parity = att.batch0 // 2 + blocks * PAIRS + pair
        self.block = blocks
        self.tile = self.batch * NT
        self.unit = att.units_before(self.tile)
        self.stores = blocks * PAIRS + pair
        self.block_a = A_K0 if att.layer == 0 else A_L1 + 2 + PER_LAYER * a + group
        self.block_b = B_V0 if att.layer == 0 else B_L1 + 2 + PER_LAYER * a + group

    def next(self):
        if self.swap:
            return Place(self.att, self.a, self.group + 1, 0, 0)
        if self.parity:
            return Place(self.att, self.a, self.group, self.pair + 1, 0, self.final_pair)
        return Place(self.att, self.a, self.group, self.pair, 1, self.final_pair)

    def key(self, t):
        if t < NT:
            return self, t
        return None if self.final else (self.next(), t - NT)

    def at(self, t, j, ahead):
        n = self.att.sub * t + j + ahead
        tile = self.key(n // self.att.sub)
        return tile and (*tile, n % self.att.sub)

    def after(self, batches):
        if batches == 0:
            return self
        return None if self.final else self.next().after(batches - 1)

    def split_column(self, t):
        return self.att.split_slots.get((self.b, t)) if isinstance(self.b, int) else None

    def split_columns_b(self, t):
        return self.att.split_slots_b.get((self.b, t), ()) if isinstance(self.b, int) else ()

    def column(self, kind, t):
        if self.att.layer == 0:
            return kind[0] + t
        return N_CB1 * self.a + kind[1] + NT * self.group + t


ATT0 = Attention(0, SUB0, 0, 0, 0)
ATT1 = Attention(1, 1, NB * NT, NB * NT * SUB0, NB)


def wait(eng, sem, value):
    if isinstance(value, int) and value <= 0:
        return
    eng.wait_ge(sem, value)


def build(nc, x_in, ctx_in, mask_in, blocks_a, blocks_b, vec_a, vec_b, value_rows, value_bias_rows, row_bias, eye, out):
    q_scr = nc.dram_tensor("q_scratch", [GROUPS, NB, P, NT * LQ], F32).ap()
    o_scr = nc.dram_tensor("o_scratch", [GROUPS, NB, P, NT * LQ], F32).ap()
    xv_scr = nc.dram_tensor("extra_value_scratch", [2, GROUPS, D], F32).ap()

    with ExitStack() as ctx:
        def sb(name, shape, dt=F32):
            return ctx.enter_context(nc.sbuf_tensor(name, shape, dt))

        def sem(name):
            return ctx.enter_context(nc.semaphore(name))

        ctx_t = sb("ctx_t", [P, DT, NB * KW])
        x = sb("x", [P, RT, D])
        ident = sb("ident", [P, P])
        col_a = sb("col_a", [P, N_CA])
        col_b = sb("col_b", [P, 2 * N_CB1])
        xk = [sb(f"xk_{s}", [P, 32], F32R) for s in ("hi", "lo")]
        bias_row = sb("bias_row", [P, D])
        mask_u8 = sb("mask_u8", [LQ, NB * LK], U8)
        key_cap = sb("key_cap", [LQ, LK])
        act_t = [sb(f"act_t_{s}", [P, DT, ROWS], F32R) for s in ("hi", "lo")]
        w_raw = [sb(f"w_raw_{s}", [P, DT, D]) for s in "ab"]
        w = [[sb(f"w_{s}_{h}", [P, DT, D], F32R) for h in ("hi", "lo")] for s in "ab"]
        cs = [[sb(f"cs{i}_{h}", [P, DT * CHUNK_MAX], F32R) for h in ("hi", "lo")] for i in range(2)]
        q = [[sb(f"q{i}_{h}", [P, NT * LQ], F32R) for h in ("hi", "lo")] for i in range(2)]
        v = [sb(f"v{i}", [P, 3, D]) for i in range(2)]
        k = [[sb(f"k{i}_{h}", [P, KW], F32R) for h in ("hi", "lo")] for i in range(2)]
        prob = [sb(f"prob{i}", [P, D]) for i in range(2)]
        prob_0 = [*prob, *(sb(f"prob{i}", [P, LK]) for i in (2, 3))]
        prob_t = [sb(f"prob_t{i}", [P, 3 * LQ]) for i in range(2)]
        o = [sb(f"o{i}", [P, D]) for i in range(2)]
        stats = sb("stats", [P, RT, 6])
        mean_var = sb("mean_var", [P, RT, 2])
        row_columns = sb("row_columns", [P, 3 * RT + 3 * 4])
        var_eps, std, rstd = (row_columns[:, i * RT:(i + 1) * RT] for i in range(3))
        max_neg, prob_sum, prob_rcp = (row_columns[:, 3 * RT + 4 * i:3 * RT + 4 * i + 4] for i in range(3))

        def bank(name):
            return ctx.enter_context(nc.psum_tensor(name, [P, 512], F32))

        ps_k, ps_v = bank("ps_k"), bank("ps_v")
        ps_s = [bank(f"ps_s{i}") for i in range(2)]
        ps_t = [bank(f"ps_t{i}") for i in range(2)]
        ps_o = [bank(f"ps_o{i}") for i in range(2)]
        ps_y = [ps_k, ps_v, *ps_o]

        vecs_in, mask_in_sem = sem("vecs_in"), sem("mask_in")
        x_in_sem = [sem(f"x_in{i}") for i in range(2)]
        ctx_in_sem = [sem("ctx_in_" + n) for n in ("first_pair", "second_pair", "others")]
        vec_t, vec_ev, vec_split, xv_diff, xv_out = (sem(n) for n in ("vec_t", "vec_ev", "vec_split", "xv_diff", "xv_out"))
        cleared = sem("cleared")
        w_in = [sem(f"w_in_{s}") for s in "ab"]
        w_hi = [sem(f"w_hi_{s}") for s in "ab"]
        w_lo = [sem(f"w_lo_{s}") for s in "ab"]
        ln_stat, ln_agg, ln_eps, ln_std, ln_rstd, ln_xhat, ln_turn, ln_act, ln_hi, ln_lo = (
            sem("ln_" + n) for n in ("stat", "agg", "eps", "std", "rstd", "xhat", "turn", "act", "hi", "lo"))
        bias_in, bias_add = sem("bias_in"), sem("bias_add")
        q_mm, q_act, q_hi, q_lo = (sem("q_" + n) for n in ("mm", "act", "hi", "lo"))
        q_out = [sem(f"q_out{i}") for i in range(4)]
        q_in = [sem(f"q_in{i}") for i in range(2)]
        cs_hi, cs_lo = sem("cs_hi"), sem("cs_lo")
        k_mm, k_hi, k_lo, k_extra = sem("k_mm"), sem("k_hi"), sem("k_lo"), sem("k_extra")
        v_mm, v_ev = sem("v_mm"), sem("v_ev")
        xv_in = [sem(f"xv_in{i}") for i in range(2)]
        s_mm, s_cap, s_max, s_exp, s_rcp, s_norm = (
            sem("s_" + n) for n in ("mm", "cap", "max", "exp", "rcp", "norm"))
        cap_half, cap_full = sem("cap_half"), sem("cap_full")
        t_mm, t_ev, av_mm = sem("t_mm"), sem("t_ev"), sem("av_mm")
        o_ev, o_hi, o_lo = sem("o_ev"), sem("o_hi"), sem("o_lo")
        o_out = [sem(f"o_out{i}") for i in range(2)]
        first_in, first_hi, first_lo = (sem("first_" + n) for n in ("in", "hi", "lo"))
        p_in = [sem(f"p_in{i}") for i in range(len(OUT_CHUNKS))]
        p_hi, p_lo = sem("p_hi"), sem("p_lo")
        y_mm, x_add = sem("y_mm"), sem("x_add")
        h_mm, h_act, h_hi, h_lo = (sem("h_" + n) for n in ("mm", "act", "hi", "lo"))
        stored = sem("stored")
        act_waited, dve_waited, pool_waited, sp_waited = (sem(n + "_waited") for n in ("act", "dve", "pool", "sp"))

        block = ctx.enter_context(nc.Block())

        def schedule(eng, ln, contexts, query, attend, project, mlp):
            ln(0, 0)
            contexts(ATT0, 0)
            query(0, 0, 0, 0, A_Q0, 0)
            attend(ATT0, 0)
            project(0, 0, 0, 1, B_O0, 0, 0)
            ln(1, RT)
            mlp(0, 0, 1, RT)
            with eng.Fori(1, 3) as fg:
                mlp(0, fg, 1, RT * (fg + 1))
            mlp(0, 3, 1, RT * 4, True)
            with eng.Fori(0, 2) as a:
                ln(2 + a, 5 * RT + 4 * RT * a)
                contexts(ATT1, a)
                with eng.Fori(0, GROUPS // 2) as half:
                    for slot, first in ((0, A_L1), (1, B_L1)):
                        query(1, a, 2 * half + slot, slot, PER_LAYER * a + half + first, 1 + 4 * a + 2 * half + slot)
                attend(ATT1, a)
                for group in range(GROUPS):
                    slot = group % 2
                    project(1, a, group, slot, PER_LAYER * a + group // 2 + (B_L1 if slot else A_L1) + 6,
                            1 + 4 * a + group, 5 * RT + 4 * RT * a + RT * group)
            ln(4, 13 * RT)
            with eng.Fori(0, 2) as fg:
                mlp(1, fg, 4, 13 * RT + RT * fg)
            mlp(1, 2, 4, 15 * RT)
            mlp(1, 3, 4, 16 * RT)

        def batches(eng, att, a, prologue, one_batch):
            def pair(group, p, final=False):
                for parity in range(2):
                    one_batch(Place(att, a, group, p, parity, final))

            prologue(Place(att, a, 0, 0, 0))
            if att.layer == 0:
                pair(0, 0)
                with eng.Fori(1, PAIRS - 1) as p:
                    pair(0, p)
                pair(0, PAIRS - 1, final=True)
                return
            with eng.Fori(0, GROUPS - 1) as group:
                with eng.Fori(0, PAIRS - 1) as p:
                    pair(group, p)
                pair(group, PAIRS - 1)
            with eng.Fori(0, PAIRS - 1) as p:
                pair(GROUPS - 1, p)
            pair(GROUPS - 1, PAIRS - 1, final=True)

        def value_parts(place, t, j):
            return ([], []) if place.final else place.att.value_parts[place.swap].get((t, j), ([], []))

        def mlp_block(m, fg):
            return (A_M0, A_M1)[m] + fg, (B_M0, B_M1)[m] + fg

        def has_pending(e):
            return not (isinstance(e, int) and e == 0)

        def pending(e):
            if isinstance(e, int) and e == 1:
                return 1, B_M0, RT
            return 1, B_L1 + PER_LAYER * (e - 2), 5 * RT + 4 * RT * (e - 2)

        def landing(c):
            return cs[c // 2][c % 2][:, 0:OUT_CHUNKS[c][1] * NT * LQ].bitcast(F32)

        def softmax_buffers(layer, t, j):
            return (t % 2, prob[t % 2]) if layer else (j, prob_0[j])

        def staged(i):
            return (prob[0], prob[1], o[0], o[1])[i % 4][:, 0:HALF]

        def split_place(part, c):
            b0, nb = OUT_CHUNKS[c]
            return act_t[part][:, :, b0 * LQ:(b0 + nb) * LQ].rearrange("p t (b r) -> p b t r", b=nb)

        def skip(*_):
            return

        def exists(slot, n):
            return not isinstance(n, int) or n < (N_A, N_B)[slot]

        def cols(att):
            return col_b if att.layer else col_a

        @block.sync
        def _(sp):
            def load_block(slot, n, columns=range(NT)):
                if not exists(slot, n):
                    return
                src = (blocks_a, blocks_b)[slot][ds(n, 1)].rearrange("o p (k n) -> (o p) k n", k=DT)
                for t in columns:
                    wait(sp, w_lo[slot], 4 * (n - 1) + t + 1)
                    part = slice(t * P, (t + 1) * P)
                    sp.dma_start(w_raw[slot][:, :, part], src[:, :, part]).then_inc(w_in[slot], 16)

            def ln(e, x0):
                wait(sp, bias_add, RT * e)
                sp.dma_start(bias_row[:], row_bias[ds(e, 1), :].partition_broadcast(P)).then_inc(bias_in, 16)
                sp.sem_inc(sp_waited, 1)
                if has_pending(e):
                    slot, n, _ = pending(e)
                    load_block(slot, n + 1)

            def contexts(att, a):
                if att.layer == 0:
                    load_block(0, 1)

            def query(layer, a, group, slot, n, step):
                for i in range(2 * NT):
                    t, half = i // 2, i % 2
                    sp.wait_ge(q_act, 8 * step + i + 1)
                    dst = q_scr[ds(group, 1), half * 4:half * 4 + 4, :, t * LQ:(t + 1) * LQ]
                    sp.dma_start(dst.rearrange("o b p r -> p (o b) r"), staged(i).rearrange("p (b r) -> p b r", b=NB // 2))\
                        .then_inc(q_out[i % 4], 16)
                    if half:
                        load_block(slot, n + 2, [t])

            def load_q(place):
                wait(sp, s_mm, place.att.units_before(place.tile - NT))
                src = q_scr[ds(place.group, 1), ds(place.b, 1)].rearrange("g b p f -> (g b p) f")
                sp.dma_start(q[place.parity][1][:].bitcast(F32), src).then_inc(q_in[place.parity], 16)

            def load_extra_value(place, buf):
                wait(sp, av_mm, place.att.units_before(place.tile - NT * (1 - buf)))
                src = xv_scr[ds(place.a, 1), ds(place.group, 1)].rearrange("a g f -> (a g) f")
                sp.dma_start(v[buf][LK - 256:LK - 255, 2, :], src).then_inc(xv_in[buf], 16)

            def attend(att, a):
                def prologue(place):
                    for i in range(4):
                        sp.wait_ge(q_out[i], 16 * 2 * (1 + 4 * (a + 1) if att.layer else 1))
                    load_q(place)
                    if att.layer == 0:
                        columns = slice(2 * KW, 4 * KW)
                        sp.dma_start(ctx_t[:, :, columns], ctx_in[:, :, columns]).then_inc(ctx_in_sem[1], 16)
                    if att.layer == 1:
                        for buf in range(2):
                            load_extra_value(place, buf)

                def one_batch(place):
                    after = None if place.final else place.next()
                    if after:
                        load_q(after)
                    if att.layer == 0 and isinstance(place.b, int) and place.b == 0:
                        sp.dma_start(ctx_t[:, :, 4 * KW:], ctx_in[:, :, 4 * KW:]).then_inc(ctx_in_sem[2], 16)
                        load_block(1, 1)
                    if place.swap:
                        if after:
                            load_extra_value(after, 0)
                        load_block(0, place.block_a + 2)
                        load_block(1, place.block_b + 2)
                    if att.layer == 0:
                        return
                    if place.last_block:
                        for i in range(2):
                            sp.wait_ge(o_out[i], 16 * place.stores)
                        sp.sem_inc(sp_waited, 1)
                        wait(sp, first_in, 16 * place.first)
                        dst = act_t[1][:, :, ds(place.b * LQ, LQ)].bitcast(F32)
                        src = o_scr[0, ds(place.b, 1)].rearrange("b p (t r) -> (b p) t r", t=NT)
                        sp.sem_inc(sp_waited, 1)
                        sp.dma_start(dst, src).then_inc(first_in, 16)
                    sp.wait_ge(o_ev, NT * place.batch + NT)
                    dst = o_scr[ds(place.group, 1), ds(place.b, 1)].rearrange("g b p f -> (g b p) f")
                    sp.dma_start(dst, o[place.parity][:, 0:NT * LQ]).then_inc(o_out[place.parity], 16)
                    if place.swap and after:
                        load_extra_value(after, 1)

                batches(sp, att, a, prologue, one_batch)

            def project(layer, a, group, slot, n, step, x0):
                for g in {0: (1, 2), 1: (3,)}.get(group, ()) if layer else ():
                    for i in range(2):
                        sp.wait_ge(o_out[i], 16 * PAIRS * GROUPS * (a + 1))
                    for c, (b0, nb) in enumerate(OUT_CHUNKS):
                        if g > 1:
                            sp.wait_ge(p_lo, 3 * (3 * a + g - 2) + c + 1)
                        src = o_scr[g, b0:b0 + nb].rearrange("b p f -> p b f")
                        sp.dma_start(landing(c).rearrange("p (b f) -> p b f", b=nb), src).then_inc(p_in[c], 16)
                if layer and group + 1 < GROUPS:
                    load_block(slot, n + 2)

            def mlp(m, fg, e, x0, last=False):
                na, nb = mlp_block(m, fg)
                load_block(0, na + 2)
                if not last:
                    load_block(1, nb + 2)
                if isinstance(fg, int) and m == 1 and fg == 3:
                    for r in range(RT):
                        sp.wait_ge(x_add, x0 + r + 1)
                        sp.dma_start(out[r * P:(r + 1) * P, :], x[:, r, :]).then_inc(stored, 16)
                    sp.wait_ge(stored, 16 * RT)

            sp.dma_start(ident[:], eye).then_inc(vecs_in, 16)
            sp.dma_start(prob[0][0:N_CA, 0:P], vec_a).then_inc(vecs_in, 16)
            sp.dma_start(prob[0][:, P:2 * P], vec_b).then_inc(vecs_in, 16)
            sp.dma_start(prob[0][0:32, 2 * P:3 * P], value_rows).then_inc(vecs_in, 16)
            sp.dma_start(prob[0][0:32, 3 * P:4 * P], value_bias_rows).then_inc(vecs_in, 16)
            for i, (r0, r1) in enumerate(X_PARTS):
                src = x_in[r0 * P:r1 * P, :].rearrange("(r p) d -> p r d", p=P)
                sp.dma_start(x[:, r0:r1, :], src).then_inc(x_in_sem[i], 16)
            sp.wait_ge(xv_diff, 1)
            sp.dma_start(xv_scr.rearrange("a g (t n) -> (a g t) n", n=P), key_cap[0:32, 0:P]).then_inc(xv_out, 16)
            sp.wait_ge(x_in_sem[1], 16)
            load_block(0, 0)
            sp.dma_start(ctx_t[:, :, 0:2 * KW], ctx_in[:, :, 0:2 * KW]).then_inc(ctx_in_sem[0], 16)
            load_block(1, 0)
            sp.dma_start(mask_u8[:], mask_in.partition_broadcast(LQ)).then_inc(mask_in_sem, 16)
            schedule(sp, ln, contexts, query, attend, project, mlp)

        @block.gpsimd
        def _(pool):
            def split_lo(slot, n, subs=range(NT)):
                if not exists(slot, n):
                    return
                for s in subs:
                    pool.wait_ge(w_hi[slot], 4 * n + s + 1)
                    part = slice(s * P, (s + 1) * P)
                    pool.tensor_tensor(w[slot][1][:, :, part], w_raw[slot][:, :, part], w[slot][0][:, :, part],
                                       ALU.subtract).then_inc(w_lo[slot], 1)

            def ln(e, x0):
                pool.wait_ge(bias_in, 16 * e + 16)
                for r in range(RT):
                    pool.wait_ge(ln_xhat, RT * e + r + 1)
                    pool.tensor_tensor(x[:, r, :], x[:, r, :], bias_row[:], ALU.add).then_inc(bias_add, 1)
                if has_pending(e):
                    split_lo(*pending(e)[0:2])

            def context_lo(place):
                pool.wait_ge(cs_hi, place.batch + 1)
                pool.tensor_tensor(cs[place.parity][1][:, 0:DT * KW].rearrange("p (k n) -> p k n", k=DT),
                                   ctx_t[:, :, ds(place.b * KW, KW)],
                                   cs[place.parity][0][:, 0:DT * KW].rearrange("p (k n) -> p k n", k=DT),
                                   ALU.subtract).then_inc(cs_lo, 1)

            def contexts(att, a):
                for parity in range(2):
                    context_lo(Place(att, a, 0, 0, parity))

            def attend(att, a):
                def extra_key(place, t):
                    col = 16 * place.a + NT * place.group + t
                    wait(pool, s_mm, att.units_before(place.tile + t - 1))
                    pool.sem_inc(pool_waited, 1)
                    pool.tensor_copy(k[t % 2][0][:, LK:KW], xk[0][:, ds(col, 1)])
                    pool.tensor_copy(k[t % 2][1][:, LK:KW], xk[1][:, ds(col, 1)]).then_inc(k_extra, 1)

                def output(place):
                    rows = ds(place.b * LQ, LQ)
                    z = o[place.parity][:, 0:NT * LQ].rearrange("p (t r) -> p t r", t=NT)
                    pool.wait_ge(o_ev, NT * place.batch + NT)
                    pool.sem_inc(pool_waited, 1)
                    pool.tensor_copy(act_t[0][:, :, rows], z).then_inc(o_hi, 1)
                    pool.wait_ge(o_hi, place.batch + 1)
                    pool.tensor_tensor(act_t[1][:, :, rows], z, act_t[0][:, :, rows], ALU.subtract).then_inc(o_lo, 1)

                def prologue(place):
                    if att.layer == 1:
                        for t in range(att.key_ahead):
                            extra_key(place, t)

                def one_batch(place):
                    for t in range(NT):
                        tile = place.key(t + att.key_ahead)
                        if att.layer == 1 and tile:
                            extra_key(*tile)
                        if t == att.context_slot[0] and place.after(2):
                            context_lo(place.after(2))
                        split_lo(1, place.block_b + 1, place.split_columns_b(t))
                    if att.layer == 0:
                        output(place)

                batches(pool, att, a, prologue, one_batch)

            def project(layer, a, group, slot, n, step, x0):
                if layer and group + 1 < GROUPS:
                    split_lo(slot, n + 1)

            def mlp(m, fg, e, x0, last=False):
                na, nb = mlp_block(m, fg)
                split_lo(0, na + 1)
                if not last:
                    split_lo(1, nb + 1)

            pool.wait_ge(w_in[0], 16 * NT)
            for s in range(4):
                part = slice(s * P, (s + 1) * P)
                pool.tensor_copy(w[0][0][:, :, part], w_raw[0][:, :, part]).then_inc(w_hi[0], 1)
            split_lo(0, 0)
            pool.wait_ge(vec_split, 2)
            schedule(pool, ln, contexts, skip, attend, project, mlp)

        @block.scalar
        def _(act):
            def split_hi(slot, n, subs, free):
                if not exists(slot, n) or not subs:
                    return
                act.wait_ge(w_in[slot], 16 * NT * (n + 1))
                for s in subs:
                    if free:
                        act.wait_ge(*free(s))
                    act.activation(w[slot][0][:, :, s * P:(s + 1) * P], w_raw[slot][:, :, s * P:(s + 1) * P],
                                   ACT.Identity).then_inc(w_hi[slot], 1)

            def ln(e, x0):
                def deviation(part, rows):
                    act.wait_ge(ln_eps, 2 * e + part + 1)
                    act.activation(std[:, rows], var_eps[:, rows], ACT.Sqrt).then_inc(ln_std, 1)

                deviation(0, slice(0, RT - 1))
                for r in range(RT):
                    act.wait_ge(ln_turn, RT * e + r + 1)
                    wait(act, ln_lo, RT * e + r - 1)
                    act.sem_inc(act_waited, 1)
                    for c in range(DT):
                        last = act.activation(o[r % 2][:, c * P:(c + 1) * P], ps_t[r % 2][:, c * P:(c + 1) * P], ACT.Identity,
                                              bias=col_a[:, ds(C_LN + 8 * e + 4 + c, 1)],
                                              scale=col_a[:, ds(C_LN + 8 * e + c, 1)])
                    last.then_inc(ln_act, 1)
                    if r == 0:
                        deviation(1, slice(RT - 1, RT))
                if has_pending(e):
                    slot, n, products = pending(e)
                    split_hi(slot, n, range(4), lambda s: (y_mm, products))
                else:
                    split_hi(1, 0, range(4), None)

            def query(layer, a, group, slot, n, step):
                scale = float((HD1 if layer else HD0) ** -0.5)
                for i in range(2 * NT):
                    t, half = i // 2, i % 2
                    col = (N_CB1 * a + C_BQ1 if layer else C_BQ0) + NT * group + t
                    act.wait_ge(q_mm, 8 * step + i + 1)
                    wait(act, q_out[i % 4], 16 * (2 * step + t // 2))
                    act.sem_inc(act_waited, 1)
                    act.activation(staged(i), ps_y[i % 4][:, 0:HALF], ACT.Identity, scale=scale,
                                   bias=(col_b if layer else col_a)[:, ds(col, 1)]).then_inc(q_act, 1)
                    if half:
                        split_hi(slot, n + 1, [t], lambda s: (q_mm, 8 * step + 2 * s + 2))

            def attend(att, a):
                sub, layer = att.sub, att.layer

                def key_hi(place, t):
                    tile = place.tile + t
                    act.wait_ge(k_mm, tile + 1)
                    wait(act, s_mm, att.units_before(tile - 1))
                    act.sem_inc(act_waited, 1)
                    n = KW if layer == 0 else LK
                    act.activation(k[t % 2][0][:, 0:n], ps_k[:, 0:n], ACT.Identity,
                                   bias=cols(att)[:, ds(place.column((C_BK0, C_BK1), t), 1)]).then_inc(k_hi, 1)

                def value(place, i):
                    n = KEY_TILES[i][1]
                    act.wait_ge(v_mm, 3 * place.batch + i + 1)
                    wait(act, av_mm, att.units_before(place.tile - NT))
                    act.activation(v[place.parity][0:n, i, :], ps_v[0:n, :], ACT.Identity).then_inc(v_ev, 1)

                def value_ends(place, parts):
                    for i, _, end in parts:
                        if end == DT:
                            value(place.next(), i)

                def turned(place, t, j):
                    unit, buf = place.unit + sub * t + j, (j if layer == 0 else t) % 2
                    act.wait_ge(t_mm, unit + 1)
                    wait(act, av_mm, unit - 1)
                    act.activation(prob_t[buf][:], ps_t[buf][:, 0:3 * LQ], ACT.Identity).then_inc(t_ev, 1)

                def exp(place, t, j):
                    unit, (col, p) = place.unit + sub * t + j, softmax_buffers(layer, t, j)
                    act.wait_ge(s_max, unit + 1)
                    if layer:
                        wait(act, t_mm, unit - 1)
                    src = ps_s[t % 2] if layer else p
                    act.activation(p[0:LQ, 0:att.keys], src[0:LQ, 0:att.keys], ACT.Exp,
                                   bias=max_neg[0:LQ, col:col + 1],
                                   accum_out=prob_sum[0:LQ, col:col + 1]).then_inc(s_exp, 1)

                def output(place, t):
                    act.wait_ge(av_mm, att.units_before(place.tile + t + 1))
                    if t == 0:
                        if layer == 0:
                            wait(act, o_lo, place.batch - 1)
                        else:
                            wait(act, o_out[place.parity], 16 * place.stores)
                    act.sem_inc(act_waited, 1)
                    act.activation(o[place.parity][:, t * LQ:(t + 1) * LQ], ps_o[t % 2][:, 0:LQ],
                                   ACT.Identity, bias=cols(att)[:, ds(place.column((C_BV0, C_BV1), t), 1)])\
                        .then_inc(o_ev, 1)

                def first_outputs(place):
                    rows = ds(place.b * LQ, LQ)
                    act.wait_ge(first_in, 16 * place.first + 16)
                    act.sem_inc(act_waited, 1)
                    act.activation(act_t[0][:, :, rows], act_t[1][:, :, rows].bitcast(F32), ACT.Identity)\
                        .then_inc(first_hi, 1)

                def split_q(place):
                    act.wait_ge(q_in[place.parity], 16 * place.same_parity + 16)
                    act.activation(q[place.parity][0][:], q[place.parity][1][:].bitcast(F32), ACT.Identity).then_inc(q_hi, 1)

                def prologue(place):
                    if layer == 0:
                        value(place, 0)
                    key_hi(place, 0)
                    if layer == 1:
                        value(place, 0)
                    key_hi(place, 1)
                    value(place, 1)
                    split_q(place)
                    value(place, 2)
                    exp(place, 0, 0)
                    if layer == 1:
                        key_hi(place, 2)
                    for unit in range(1, att.exp_ahead):
                        exp(*place.at(0, 0, unit))
                    turned(place, 0, 0)

                def one_batch(place):
                    for t in range(NT):
                        for j in range(sub):
                            value_ends(place, value_parts(place, t, j)[0])
                            next_key = place.key(t + att.key_ahead) if j == att.key_slot else None
                            if next_key and layer == 1:
                                key_hi(*next_key)
                            if place.at(t, j, 1):
                                turned(*place.at(t, j, 1))
                            if place.at(t, j, att.exp_ahead):
                                exp(*place.at(t, j, att.exp_ahead))
                            if next_key and layer == 0:
                                key_hi(*next_key)
                            if j == sub - 1 and place.split_column(t) is not None:
                                split_hi(0, place.block_a + 1, [place.split_column(t)],
                                         lambda s: (k_mm, place.tile + NT * (1 - place.parity) + s + 1))
                            if j == sub - 1:
                                output(place, t)
                            value_ends(place, value_parts(place, t, j)[1])
                            if (t, j) == att.query_slot and not place.final:
                                split_q(place.next())
                            if j == 0:
                                split_hi(1, place.block_b + 1, place.split_columns_b(t),
                                         lambda s: (v_mm, 3 * (place.batch + 1 - place.parity) + 3))
                            if place.last_block and t == 2:
                                first_outputs(place)

                batches(act, att, a, prologue, one_batch)

            def project(layer, a, group, slot, n, step, x0):
                if layer and group + 1 < GROUPS:
                    for c in range(len(OUT_CHUNKS)):
                        act.wait_ge(p_in[c], 16 * (3 * a + group + 1))
                        act.wait_ge(y_mm, x0 + CHUNK_FREE[c])
                        act.activation(split_place(0, c), landing(c).rearrange("p (b t r) -> p b t r", t=NT, r=LQ),
                                       ACT.Identity).then_inc(p_hi, 1)
                if layer and group + 1 < GROUPS:
                    split_hi(slot, n + 1, range(4), lambda s: (y_mm, x0 + RT))

            def mlp(m, fg, e, x0, last=False):
                na, nb = mlp_block(m, fg)
                for c, (r0, nr) in enumerate(MLP_CHUNKS):
                    for f in range(4):
                        u = 12 * (4 * m + fg) + 4 * c + f
                        col = (C_FC0, C_FC1)[m] + 4 * fg + f
                        act.wait_ge(h_mm, u + 1)
                        wait(act, h_lo, u - 1)
                        act.sem_inc(act_waited, 1)
                        act.activation(prob[f % 2][:, 0:nr], ps_s[f % 2][:, 0:nr],
                                       ACT.Gelu if m else ACT.Gelu_apprx_tanh,
                                       bias=col_a[:, ds(col, 1)]).then_inc(h_act, 1)
                split_hi(0, na + 1, range(4), lambda s: (h_mm, 12 * (4 * m + fg) + 8 + s + 1))
                if not last:
                    split_hi(1, nb + 1, range(4), lambda s: (y_mm, x0 + RT))

            act.wait_ge(vec_ev, 4)
            schedule(act, ln, skip, query, attend, project, mlp)

        @block.vector
        def _(dve):
            def split_lo(slot, n, subs):
                if not exists(slot, n):
                    return
                for s in subs:
                    dve.wait_ge(w_hi[slot], 4 * n + s + 1)
                    part = slice(s * P, (s + 1) * P)
                    dve.tensor_tensor(w[slot][1][:, :, part], w_raw[slot][:, :, part], w[slot][0][:, :, part],
                                      ALU.subtract).then_inc(w_lo[slot], 1)

            def statistics(r, e):
                dve.bn_stats(stats[:, r, :], x[:, r, :]).then_inc(ln_stat, 1)
                if 0 < r < RT - 1:
                    mean_variance(r - 1, e)

            def mean_variance(r, e):
                dve.wait_ge(ln_stat, RT * e + r + 1)
                dve.sem_inc(dve_waited, 1)
                dve.bn_aggr(mean_var[:, r, :], stats[:, r, :]).then_inc(ln_agg, 1)

            def variance_eps(rows, e):
                dve.wait_ge(ln_agg, RT * e + rows.stop)
                dve.tensor_scalar(var_eps[:, rows], mean_var[:, rows, 1], EPS, None, ALU.add).then_inc(ln_eps, 1)

            def deviation(part, rows, e):
                dve.wait_ge(ln_std, 2 * e + part + 1)
                dve.reciprocal(rstd[:, rows], std[:, rows]).then_inc(ln_rstd, 1)
                dve.wait_ge(ln_rstd, 2 * e + part + 1)

            def normalized(r, e):
                wait(dve, ln_turn, RT * e + r - 1)
                dve.tensor_scalar(prob[r % 2][:], x[:, r, :], mean_var[:, r, 0:1], rstd[:, r:r + 1],
                                  ALU.subtract, ALU.mult).then_inc(ln_xhat, 1)

            def ln_head(e):
                mean_variance(RT - 2, e)
                variance_eps(slice(0, RT - 1), e)
                deviation(0, slice(0, RT - 1), e)
                normalized(0, e)
                normalized(1, e)

            def ln(e, x0):
                if isinstance(e, int) and e == 0:
                    for r in range(RT - 1):
                        for i, (r0, _) in enumerate(X_PARTS):
                            if r == r0:
                                dve.wait_ge(x_in_sem[i], 16)
                        statistics(r, e)
                    ln_head(e)
                    statistics(RT - 1, e)
                for r in range(RT):
                    if r == 1:
                        deviation(1, slice(RT - 1, RT), e)
                    if r + 2 < RT:
                        normalized(r + 2, e)
                    if r == 0:
                        mean_variance(RT - 1, e)
                        variance_eps(slice(RT - 1, RT), e)
                    z = o[r % 2][:].rearrange("p (k n) -> p k n", k=DT)
                    dve.wait_ge(ln_act, RT * e + r + 1)
                    dve.tensor_copy(act_t[0][:, :, r * P:(r + 1) * P], z).then_inc(ln_hi, 1)
                    dve.wait_ge(ln_hi, RT * e + r + 1)
                    dve.tensor_tensor(act_t[1][:, :, r * P:(r + 1) * P], z, act_t[0][:, :, r * P:(r + 1) * P],
                                      ALU.subtract).then_inc(ln_lo, 1)
                if isinstance(e, int) and e == 0:
                    split_lo(1, 0, range(4))

            def query(layer, a, group, slot, n, step):
                for t in range(NT):
                    split_lo(slot, n + 1, [t])

            def context_hi(place):
                if place.att.layer == 0:
                    pair = place.pair if isinstance(place.pair, int) else 2
                    dve.wait_ge(ctx_in_sem[min(pair, 2)], 16)
                dve.tensor_copy(cs[place.parity][0][:, 0:DT * KW].rearrange("p (k n) -> p k n", k=DT),
                                ctx_t[:, :, ds(place.b * KW, KW)]).then_inc(cs_hi, 1)

            def contexts(att, a):
                if att.layer:
                    dve.wait_ge(y_mm, 5 * RT + 4 * RT * a)
                for parity in range(2):
                    context_hi(Place(att, a, 0, 0, parity))

            def attend(att, a):
                sub, layer = att.sub, att.layer

                def split_q(place):
                    dve.wait_ge(q_hi, place.batch + 1)
                    dve.tensor_tensor(q[place.parity][1][:], q[place.parity][1][:].bitcast(F32), q[place.parity][0][:],
                                      ALU.subtract).then_inc(q_lo, 1)

                def key_lo(place, t):
                    n = KW if layer == 0 else LK
                    dve.wait_ge(k_hi, place.tile + t + 1)
                    dve.scalar_tensor_tensor(out=k[t % 2][1][:, 0:n], in0=ps_k[:, 0:n],
                                             scalar=cols(att)[:, ds(place.column((C_BK0, C_BK1), t), 1)],
                                             in1=k[t % 2][0][:, 0:n], op0=ALU.add, op1=ALU.subtract).then_inc(k_lo, 1)

                def key_caps(place):
                    dve.tensor_scalar(key_cap[:], mask_u8[:, ds(place.b * LK, LK)], -0.5, LARGEST,
                                      ALU.add, ALU.mult).then_inc(cap_half, 1)
                    dve.wait_ge(cap_half, place.batch + 1)
                    dve.tensor_scalar(key_cap[:], key_cap[:], 2.0, None, ALU.mult).then_inc(cap_full, 1)
                    dve.wait_ge(cap_full, place.batch + 1)

                def capped(place, t, j):
                    unit = place.unit + sub * t + j
                    if (t, j) == (0, 0):
                        key_caps(place)
                    dve.wait_ge(s_mm, unit + 1)
                    wait(dve, t_mm, unit - SUB0 + 1)
                    dve.tensor_tensor(prob_0[j][0:LQ, 0:LK], ps_s[j % 2][0:LQ, 0:LK], key_cap[:], ALU.min).then_inc(s_cap, 1)

                def maximum(place, t, j):
                    unit, (col, p) = place.unit + sub * t + j, softmax_buffers(layer, t, j)
                    if layer:
                        dve.wait_ge(s_mm, unit + 1)
                        src = ps_s[t % 2][0:LQ, 0:KW]
                    else:
                        dve.wait_ge(s_cap, unit + 1)
                        src = p[0:LQ, 0:LK]
                    dve.tensor_reduce(max_neg[0:LQ, col:col + 1], src, AX_X, ALU.max, negate=True).then_inc(s_max, 1)

                def normalize(place, t, j):
                    unit, (col, p) = place.unit + sub * t + j, softmax_buffers(layer, t, j)
                    dve.wait_ge(s_exp, unit + 1)
                    dve.reciprocal(prob_rcp[0:LQ, col:col + 1], prob_sum[0:LQ, col:col + 1]).then_inc(s_rcp, 1)
                    dve.wait_ge(s_rcp, unit + 1)
                    dve.tensor_scalar(p[0:LQ, 0:att.keys], p[0:LQ, 0:att.keys],
                                      prob_rcp[0:LQ, col:col + 1], None, ALU.mult).then_inc(s_norm, 1)

                def first_outputs(place):
                    rows = ds(place.b * LQ, LQ)
                    dve.wait_ge(first_hi, place.first + 1)
                    dve.tensor_tensor(act_t[1][:, :, rows], act_t[1][:, :, rows].bitcast(F32), act_t[0][:, :, rows],
                                      ALU.subtract).then_inc(first_lo, 1)

                def prologue(place):
                    if layer == 0:
                        dve.wait_ge(xv_out, 16)
                        dve.wait_ge(mask_in_sem, 16)
                    key_lo(place, 0)
                    key_lo(place, 1)
                    split_q(place)
                    if layer == 0:
                        for j in range(SUB0):
                            capped(place, 0, j)
                            maximum(place, 0, j)
                            if j in (1, 2):
                                normalize(place, 0, j - 1)
                    else:
                        maximum(place, 0, 0)
                        normalize(place, 0, 0)
                        key_lo(place, 2)
                        maximum(place, 1, 0)
                        normalize(place, 1, 0)

                def one_batch(place):
                    for t in range(NT):
                        for j in range(sub):
                            two_on = place.at(t, j, 2)
                            to_score = place.at(t, j, att.score_ahead)
                            next_key = place.key(t + att.key_ahead) if j == att.key_slot else None
                            if layer == 0:
                                if two_on:
                                    normalize(*two_on)
                                if to_score:
                                    capped(*to_score)
                                    maximum(*to_score)
                                if next_key:
                                    key_lo(*next_key)
                            else:
                                if next_key:
                                    key_lo(*next_key)
                                if to_score:
                                    maximum(*to_score)
                                    normalize(*two_on)
                            if j == sub - 1 and place.split_column(t) is not None:
                                split_lo(0, place.block_a + 1, [place.split_column(t)])
                            if (t, j) == att.query_slot and not place.final:
                                split_q(place.next())
                            if (t, j) == att.context_slot and place.after(2):
                                wait(dve, k_mm, place.after(2).tile - NT)
                                context_hi(place.after(2))
                            if place.last_block and t == 2:
                                first_outputs(place)

                batches(dve, att, a, prologue, one_batch)

            def add_y(r, e, x0, last):
                if last and r == RT - 1:
                    ln_head(e + 1)
                dve.wait_ge(y_mm, x0 + r + 1)
                dve.wait_ge(bias_add, RT * e + r + 1)
                wait(dve, x_add, x0 + r + 1 - RT)
                dve.tensor_tensor(x[:, r, :], ps_y[r % 4][:], x[:, r, :], ALU.add).then_inc(x_add, 1)
                if last:
                    dve.wait_ge(x_add, x0 + r + 1)
                    statistics(r, e + 1)

            def project(layer, a, group, slot, n, step, x0):
                more = layer and group + 1 < GROUPS
                for r in range(RT):
                    add_y(r, 2 + a if layer else 0, x0, not more)
                    if more and r + 1 in CHUNK_FREE:
                        c = CHUNK_FREE.index(r + 1)
                        dve.wait_ge(p_hi, 3 * (3 * a + group) + c + 1)
                        dve.tensor_tensor(split_place(1, c), landing(c).rearrange("p (b t r) -> p b t r", t=NT, r=LQ),
                                          split_place(0, c), ALU.subtract).then_inc(p_lo, 1)

            def mlp(m, fg, e, x0, last=False):
                na, nb = mlp_block(m, fg)

                def hidden(c):
                    r0, nr = MLP_CHUNKS[c]
                    wait(dve, y_mm, x0 + MLP_CHUNKS[0][1] // P if c == 2 else x0)
                    for f in range(4):
                        u = 12 * (4 * m + fg) + 4 * c + f
                        hi, lo = (cs[c % 2][s][:, f * CHUNK_MAX:f * CHUNK_MAX + nr] for s in range(2))
                        dve.wait_ge(h_act, u + 1)
                        dve.tensor_copy(hi, prob[f % 2][:, 0:nr]).then_inc(h_hi, 1)
                        dve.wait_ge(h_hi, u + 1)
                        dve.tensor_tensor(lo, prob[f % 2][:, 0:nr], hi, ALU.subtract).then_inc(h_lo, 1)

                def add_chunk(c):
                    r0, nr = MLP_CHUNKS[c]
                    for r in range(r0 // P, (r0 + nr) // P):
                        add_y(r, e, x0, last)

                hidden(0)
                hidden(1)
                add_chunk(0)
                hidden(2)
                add_chunk(1)
                add_chunk(2)

            for i in range(2):
                last = dve.memset(ps_t[i][:], 0.0)
            last.then_inc(cleared, 1)
            dve.wait_ge(vec_t, 1)
            dve.wait_ge(cleared, 1)
            dve.tensor_scalar(col_a[:, 0:NT], ps_t[0][:, 0:NT], float(HD0 ** -0.5), None, ALU.mult).then_inc(vec_ev, 1)
            dve.tensor_copy(col_a[:, NT:N_CA], ps_t[0][:, NT:N_CA]).then_inc(vec_ev, 1)
            by_layer = [t.rearrange("p (a c) -> p a c", a=2) for t in (col_b[:], ps_t[1][:, 0:P])]
            dve.tensor_scalar(by_layer[0][:, :, 0:16], by_layer[1][:, :, 0:16], float(HD1 ** -0.5), None,
                              ALU.mult).then_inc(vec_ev, 1)
            dve.tensor_copy(by_layer[0][:, :, 16:N_CB1], by_layer[1][:, :, 16:N_CB1]).then_inc(vec_ev, 1)
            dve.wait_ge(vec_ev, 4)
            extra = [t.rearrange("p (a c) -> p a c", a=2) for t in (xk[0][:], xk[1][:])]
            dve.tensor_copy(extra[0], by_layer[0][:, :, C_XK1:N_CB1]).then_inc(vec_split, 1)
            dve.wait_ge(vec_split, 1)
            dve.tensor_tensor(extra[1], by_layer[0][:, :, C_XK1:N_CB1], extra[0], ALU.subtract).then_inc(vec_split, 1)
            dve.wait_ge(vecs_in, 16 * 5)
            dve.tensor_tensor(key_cap[0:32, 0:P], prob[0][0:32, 2 * P:3 * P], prob[0][0:32, 3 * P:4 * P],
                              ALU.subtract).then_inc(xv_diff, 1)
            schedule(dve, ln, contexts, query, attend, project, mlp)

        @block.tensor
        def _(pe):
            def product(out, stationary, moving, first, last):
                (w_h, w_l), (m_h, m_l) = stationary, moving
                pe.matmul(out, w_h, m_h, start=first, stop=False)
                pe.matmul(out, w_h, m_l, start=False, stop=False)
                return pe.matmul(out, w_l, m_h, start=False, stop=last)

            def ln(e, x0):
                for r in range(RT):
                    pe.wait_ge(ln_xhat, RT * e + r + 1)
                    wait(pe, ln_act, RT * e + r - 1)
                    if isinstance(e, int) and e == 0:
                        pe.wait_ge(vec_ev, 4)
                    for c in range(DT):
                        last = pe.transpose(ps_t[r % 2][:, c * P:(c + 1) * P], prob[r % 2][:, c * P:(c + 1) * P], ident[:])
                    last.then_inc(ln_turn, 1)

            def query(layer, a, group, slot, n, step):
                for i in range(2 * NT):
                    t, half = i // 2, i % 2
                    if t == 0:
                        pe.wait_ge(ln_lo, RT * (2 + a if layer else 0) + (RT if half else -(-HALF // P)))
                    pe.wait_ge(w_lo[slot], 4 * n + t + 1)
                    wait(pe, q_act, 8 * step + i - 3)
                    for c in range(DT):
                        last = product(ps_y[i % 4][:, 0:HALF],
                                       [w[slot][s][:, c, t * P:(t + 1) * P] for s in range(2)],
                                       [act_t[s][:, c, half * HALF:(half + 1) * HALF] for s in range(2)],
                                       c == 0, c == DT - 1)
                    last.then_inc(q_mm, 1)

            def attend(att, a):
                sub, layer = att.sub, att.layer

                def context_ready(place):
                    pe.wait_ge(cs_hi, place.batch + 1)
                    pe.wait_ge(cs_lo, place.batch + 1)

                def key(place, t, part=(0, DT)):
                    tile = place.tile + t
                    if part[0] == 0:
                        if t == 0:
                            context_ready(place)
                        pe.wait_ge(w_lo[0], 4 * place.block_a + t + 1)
                        wait(pe, k_lo, tile)
                    for c in range(*part):
                        last = product(ps_k[:, 0:KW],
                                       [w[0][s][:, c, t * P:(t + 1) * P] for s in range(2)],
                                       [cs[place.parity][s][:, c * KW:(c + 1) * KW] for s in range(2)],
                                       c == 0, c == DT - 1)
                    if part[1] == DT:
                        last.then_inc(k_mm, 1)

                def value(place, i, start=0, end=DT):
                    if start == 0:
                        if i == 0:
                            context_ready(place)
                            pe.wait_ge(w_lo[1], 4 * place.block_b + 4)
                        wait(pe, v_ev, 3 * place.batch + i)
                    k0, n = KEY_TILES[i]
                    for c in range(start, end):
                        last = product(ps_v[0:n, :],
                                       [cs[place.parity][s][:, c * KW + k0:c * KW + k0 + n] for s in range(2)],
                                       [w[1][s][:, c, :] for s in range(2)], c == 0, c == DT - 1)
                    if end == DT:
                        last.then_inc(v_mm, 1)

                def scores(place, t, j):
                    unit, buf = place.unit + sub * t + j, (j if layer == 0 else t) % 2
                    if j == 0:
                        pe.wait_ge(k_lo, place.tile + t + 1)
                        if layer:
                            pe.wait_ge(k_extra, place.tile + t + 1 - att.tile0)
                    if (t, j) == (0, 0):
                        pe.wait_ge(q_lo, place.batch + 1)
                    wait(pe, s_exp if layer else s_cap, unit - 1)
                    rows = slice(0, P) if layer else slice(HD0 * j, HD0 * (j + 1))
                    product(ps_s[buf][0:LQ, 0:KW],
                            [q[place.parity][s][rows, t * LQ:(t + 1) * LQ] for s in range(2)],
                            [k[t % 2][s][rows, :] for s in range(2)], True, True).then_inc(s_mm, 1)

                def turn(place, t, j):
                    unit, buf = place.unit + sub * t + j, (j if layer == 0 else t) % 2
                    p = softmax_buffers(layer, t, j)[1]
                    pe.wait_ge(s_norm, unit + 1)
                    wait(pe, t_ev, unit - 1)
                    for i, n in enumerate(att.vals()):
                        last = pe.transpose(ps_t[buf][0:n, i * LQ:(i + 1) * LQ],
                                            p[0:LQ, i * P:i * P + n], ident[0:LQ, 0:LQ])
                    last.then_inc(t_mm, 1)

                def weighted(place, t, j):
                    unit, buf = place.unit + sub * t + j, (j if layer == 0 else t) % 2
                    if (t, j) == (0, 0):
                        pe.wait_ge(v_ev, 3 * place.batch + 3)
                        if layer:
                            pe.wait_ge(xv_in[place.parity], 16 * place.block + 16)
                    if j == 0:
                        wait(pe, o_ev, NT * place.batch + t - 1)
                    pe.wait_ge(t_ev, unit + 1)
                    rows = slice(0, P) if layer else slice(HD0 * j, HD0 * (j + 1))
                    for i, n in enumerate(att.vals()):
                        last = pe.matmul(ps_o[t % 2][rows, 0:LQ],
                                         v[place.parity][0:n, i, t * P + rows.start:t * P + rows.stop],
                                         prob_t[buf][0:n, i * LQ:(i + 1) * LQ], start=(i == 0), stop=(i == 2))
                    last.then_inc(av_mm, 1)

                def prologue(place):
                    pe.wait_ge(q_act, 8 * (1 + 4 * (a + 1) if layer else 1) - 2)
                    if layer == 0:
                        value(place, 0)
                    key(place, 0)
                    if layer == 1:
                        value(place, 0)
                    key(place, 1)
                    value(place, 1)
                    pe.wait_ge(q_act, 8 * (1 + 4 * (a + 1) if layer else 1))
                    value(place, 2)
                    scores(place, 0, 0)
                    if layer == 1:
                        key(place, 2)
                    for unit in range(1, att.score_ahead):
                        scores(*place.at(0, 0, unit))
                    turn(place, 0, 0)

                def one_batch(place):
                    for t in range(NT):
                        for j in range(sub):
                            for part in value_parts(place, t, j)[0]:
                                value(place.next(), *part)
                            if j in att.key_parts and place.key(t + att.key_ahead):
                                key(*place.key(t + att.key_ahead), att.key_parts[j])
                            if place.at(t, j, 1):
                                turn(*place.at(t, j, 1))
                            if place.at(t, j, att.score_ahead):
                                scores(*place.at(t, j, att.score_ahead))
                            weighted(place, t, j)
                            for part in value_parts(place, t, j)[1]:
                                value(place.next(), *part)

                batches(pe, att, a, prologue, one_batch)

            def bank_read(r, x0):
                before = r - 4 if r >= 4 else (r + 4 if r + 4 < RT else r) - RT
                wait(pe, x_add, x0 + before + 1)

            def project(layer, a, group, slot, n, step, x0):
                pe.wait_ge(w_lo[slot], 4 * n + 4)
                for r in range(RT):
                    if group == 0:
                        pe.wait_ge(first_lo if layer else o_lo, NB * a + -(-(r + 1) * P // LQ))
                    if group == 0 and r == 2:
                        pe.wait_ge(o_ev, NT * NB * (1 + GROUPS * (a + 1) if layer else 1))
                    if layer and group:
                        pe.wait_ge(p_lo, 3 * (3 * a + group - 1) + CHUNK_OF[r] + 1)
                    bank_read(r, x0)
                    for t in range(NT):
                        last = product(ps_y[r % 4][:], [act_t[s][:, t, r * P:(r + 1) * P] for s in range(2)],
                                       [w[slot][s][:, t, :] for s in range(2)], t == 0, t == NT - 1)
                    last.then_inc(y_mm, 1)

            def mlp(m, fg, e, x0, last=False):
                na, nb = mlp_block(m, fg)

                def up(c):
                    r0, nr = MLP_CHUNKS[c]
                    pe.wait_ge(ln_lo, RT * e + (r0 + nr) // P)
                    for f in range(4):
                        u = 12 * (4 * m + fg) + 4 * c + f
                        pe.wait_ge(w_lo[0], 4 * na + f + 1)
                        wait(pe, h_act, u - 1)
                        for t in range(DT):
                            last = product(ps_s[f % 2][:, 0:nr], [w[0][s][:, t, f * P:(f + 1) * P] for s in range(2)],
                                           [act_t[s][:, t, r0:r0 + nr] for s in range(2)], t == 0, t == DT - 1)
                        last.then_inc(h_mm, 1)

                def down(c):
                    r0, nr = MLP_CHUNKS[c]
                    pe.wait_ge(h_lo, 12 * (4 * m + fg) + 4 * c + 4)
                    pe.wait_ge(w_lo[1], 4 * nb + 4)
                    for i in range(nr // P):
                        r = r0 // P + i
                        bank_read(r, x0)
                        for f in range(4):
                            at = f * CHUNK_MAX + i * P
                            last = product(ps_y[r % 4][:], [cs[c % 2][s][:, at:at + P] for s in range(2)],
                                           [w[1][s][:, f, :] for s in range(2)], f == 0, f == 3)
                        last.then_inc(y_mm, 1)

                up(0)
                up(1)
                down(0)
                up(2)
                down(1)
                down(2)

            pe.wait_ge(vecs_in, 16 * 5)
            pe.wait_ge(cleared, 1)
            pe.transpose(ps_t[0][:, 0:N_CA], prob[0][0:N_CA, 0:P], ident[0:N_CA, 0:N_CA])
            pe.transpose(ps_t[1][:, 0:P], prob[0][:, P:2 * P], ident[:]).then_inc(vec_t, 1)
            schedule(pe, ln, skip, query, attend, project, mlp)


def kernel(**inputs):
    import numpy as np
    import concourse.bacc as bacc
    from concourse.bass_utils import run_bass_kernel_spmd

    g = {name: np.asarray(value) for name, value in inputs.items()}
    l0, l1 = (lambda n: g["L0_xattn_" + n]), (lambda n: g["L1_xattn_" + n])

    def blocks(weight):
        rows, columns = weight.shape
        if rows == D:
            b = weight.reshape(DT, P, columns // D, D).transpose(2, 1, 0, 3)
        else:
            b = weight.reshape(rows // D, DT, P, D).transpose(0, 2, 1, 3)
        return list(b.reshape(-1, P, DT * D))

    a = blocks(l0("q_w")) + blocks(l0("k_w")) + blocks(l0("fc_w"))
    b = blocks(l0("v_w")) + blocks(l0("cproj_w")) + blocks(l0("proj_w"))
    for i in "12":
        wq, wk, wv, wo = (blocks(l1(f"w{m}{i}")) for m in "qkvo")
        a += wq[0::2] + wk + wo[0::2]
        b += wq[1::2] + wv + wo[1::2]
    a += blocks(l1("w_fc1"))
    b += blocks(l1("w_fc2"))
    blocks_a, blocks_b = np.stack(a), np.stack(b)

    def rows(*names):
        return np.concatenate([g[n].reshape(-1, P) for n in names])

    vec_a = rows("L0_xattn_q_b", "L0_xattn_k_b", "L0_xattn_v_b", "L0_xattn_fc_b", "L1_xattn_b_fc1",
                 "L0_xattn_ln1_w", "L0_xattn_ln1_b", "L0_xattn_ln2_w", "L0_xattn_ln2_b",
                 "L1_xattn_ln1_scale", "L1_xattn_ln1_offset", "L1_xattn_ln2_scale", "L1_xattn_ln2_offset",
                 "L1_xattn_ln_mlp_scale", "L1_xattn_ln_mlp_offset")
    vec_b = rows(*(f"L1_xattn_{n}{i}" for i in "12" for n in ("bq", "bk", "bv", "bias_k")))
    ctx = np.zeros((P, DT, NB, KW), g["ctx_2048"].dtype)
    ctx[:, :, :, 0:LK] = g["ctx_2048"].transpose(2, 0, 1).reshape(DT, P, NB, LK).transpose(1, 0, 2, 3)
    arrays = {
        "x": g["x"].reshape(ROWS, D),
        "ctx_t": ctx.reshape(P, DT, NB * KW),
        "mask": g["mask_BxS2_bf1"].reshape(1, NB * LK).view(np.uint8),
        "blocks_a": blocks_a, "blocks_b": blocks_b, "vec_a": vec_a, "vec_b": vec_b,
        "value_rows": rows("L1_xattn_bias_v1", "L1_xattn_bias_v2"),
        "value_bias_rows": rows("L1_xattn_bv1", "L1_xattn_bv2"),
        "row_bias": np.stack([l0("cproj_b"), l0("proj_b"), l1("bo1"), l1("bo2"), l1("b_fc2")]),
        "eye": np.eye(P, dtype=np.float32),
    }
    nc = bacc.Bacc("TRN2", target_bir_lowering=False, num_devices=1)
    arrays = {f"in_{n}": np.ascontiguousarray(v) for n, v in arrays.items()}
    args = [nc.dram_tensor(n, v.shape, mybir.dt.from_np(v.dtype), kind="ExternalInput").ap() for n, v in arrays.items()]
    out = nc.dram_tensor("out", (ROWS, D), F32, kind="ExternalOutput").ap()
    build(nc, *args, out)
    result = run_bass_kernel_spmd(nc, [arrays], core_ids=[0])
    return result.results[0]["out"].reshape(NB, LQ, D)
```
